# Optimizing a Trainium2 kernel written in Bass

```python
import numpy as np
import jax
import jax.numpy as jnp

def _softmax(x, axis=-1):
    return jax.nn.softmax(x, axis=axis)

def _gelu(x):
    return jax.nn.gelu(x, approximate=True)

def _silu(x):
    return jax.nn.silu(x)

def _sigmoid(x):
    return jax.nn.sigmoid(x)

def _layernorm(x, axis=-1, eps=1e-05):
    m = jnp.mean(x, axis=axis, keepdims=True)
    v = jnp.var(x, axis=axis, keepdims=True)
    return (x - m) / jnp.sqrt(v + eps)

def _scatter_add(tgt, idx, src, axis=0):
    return tgt.at[idx].add(src)

def _segment_sum(src, seg, n):
    return jax.ops.segment_sum(src, seg, n)
kernel_name = 'mk_flamingo_gated_d1_seqx_r4_bb9a1c'

def setup_inputs(seed: int=0):
    np.random.seed(seed)
    _w = jnp.asarray

    def _rec_inputs():
        import jax
        import jax.numpy as jnp
        _rk = jax.random.key(seed)
        x = -0.0002928 + 1 * jax.random.normal(jax.random.fold_in(_rk, 1), (4, 1024, 256), jnp.float32)
        _lenS = 1024 - jax.random.randint(jax.random.fold_in(_rk, 7), (4,), 0, max(1, 1024 // 4) + 1, jnp.int32)
        _lenS2 = 154 - jax.random.randint(jax.random.fold_in(_rk, 8), (4,), 0, max(1, 154 // 4) + 1, jnp.int32)
        _ctx_1024P = jax.random.normal(jax.random.fold_in(_rk, 11), (4, 16, 256), jnp.float32)
        _ctx_1024c = jax.random.dirichlet(jax.random.fold_in(_rk, 511), 0.3 * jnp.ones((16,), jnp.float32), (4, 154))
        _ctx_1024t = jnp.einsum('bsk,bkd->bsd', _ctx_1024c, _ctx_1024P)
        _ctx_1024t = _ctx_1024t * jax.lax.rsqrt(jnp.mean(jnp.square(_ctx_1024t)) + 1e-12) * 0.953939
        ctx_1024 = 2.81802e-05 + 1.00001 * (_ctx_1024t + 0.3 * jax.random.normal(jax.random.fold_in(_rk, 611), (4, 154, 256), jnp.float32))
        _validS = jnp.arange(1024)[None, :] < _lenS[:, None]
        _validS2 = jnp.arange(154)[None, :] < _lenS2[:, None]
        _causal = jnp.tril(jnp.ones((1024, 1024), dtype=bool))
        mask_BxS2_bk0 = jnp.logical_not(jnp.broadcast_to(_validS2[:, :], (4, 154)))
        _g = jax.random.normal(jax.random.fold_in(_rk, 9001), (2, 1), jnp.float32)
        _g = jnp.sign(_g) * jnp.maximum(jnp.abs(_g), 1.0) + (_g == 0) * 1.0
        g_xattn = _g[0]
        g_ffn = _g[1]
        return (x, ctx_1024, mask_BxS2_bk0, g_xattn, g_ffn)
    x, ctx_1024, mask_BxS2_bk0, g_xattn, g_ffn = _rec_inputs()

    def _L0_xattn_setup():
        import jax, jax.numpy as jnp
        import numpy as np
        NUM_HEADS, NUM_KV, HEAD_DIM, WIDTH = (4, 1, 64, 256)
        MASK_FILL = -2.3819763e+38

        def _apply_rope(x, positions, max_wavelength=10000.0):
            d = x.shape[-1]
            freq_exp = 2.0 / d * jnp.arange(d // 2, dtype=jnp.float32)
            timescale = max_wavelength ** freq_exp
            radians = positions[..., None].astype(jnp.float32) / timescale
            radians = radians[..., None, :]
            sin, cos = (jnp.sin(radians), jnp.cos(radians))
            x1, x2 = jnp.split(x, 2, axis=-1)
            out = jnp.concatenate([x1 * cos - x2 * sin, x2 * cos + x1 * sin], axis=-1)
            return out.astype(x.dtype)

        def _rmsnorm(x, scale):
            var = jnp.mean(jnp.square(x.astype(jnp.float32)), axis=-1, keepdims=True)
            normed = x * jax.lax.rsqrt(var + 1e-06)
            return (normed * (1 + scale)).astype(x.dtype)
        key = jax.random.key(seed)
        ks = jax.random.split(key, 7)
        B, T, S = (8, 128, 512)
        return {'x': jax.random.normal(ks[0], (B, T, WIDTH), jnp.float32), 'mem_seq': jax.random.normal(ks[1], (B, S, WIDTH), jnp.float32), 'mem_mask': jax.random.randint(ks[2], (B, S), 0, 2).astype(bool), 'rms_scale': jax.random.normal(ks[3], (WIDTH,), jnp.float32) * 0.02, 'q_w': jax.random.normal(ks[4], (NUM_HEADS, WIDTH, HEAD_DIM), jnp.float32) / np.sqrt(WIDTH), 'kv_w': jax.random.normal(ks[5], (2, NUM_KV, WIDTH, HEAD_DIM), jnp.float32) / np.sqrt(WIDTH), 'out_w': jax.random.normal(ks[6], (NUM_HEADS, HEAD_DIM, WIDTH), jnp.float32) / np.sqrt(NUM_HEADS * HEAD_DIM)}
    _L0_xattn_all = _L0_xattn_setup()
    _L0_xattn_in = {k: v for k, v in _L0_xattn_all.items() if k in ('rms_scale', 'q_w', 'kv_w', 'out_w')}
    del _L0_xattn_all

    def _L0_ffn_setup():
        import jax, jax.numpy as jnp
        import numpy as np
        EMB = 256
        FF = 4 * EMB

        def _ternary(w):
            scale = jnp.maximum(jnp.mean(jnp.abs(w)), 1e-08)
            w_t = jnp.clip(jnp.round(w / scale), -1.0, 1.0)
            return w + jax.lax.stop_gradient(w_t - w)
        key = jax.random.key(seed)
        kx, k1, k2, kb1, kb2 = jax.random.split(key, 5)
        x = jax.random.normal(kx, (4, 512, EMB), dtype=jnp.float32)
        lim1 = 1.0 / np.sqrt(EMB)
        lim2 = 1.0 / np.sqrt(FF)
        W1 = jax.random.uniform(k1, (FF, EMB), jnp.float32, -lim1, lim1)
        b1 = jax.random.uniform(kb1, (FF,), jnp.float32, -lim1, lim1)
        W2 = jax.random.uniform(k2, (EMB, FF), jnp.float32, -lim2, lim2)
        b2 = jax.random.uniform(kb2, (EMB,), jnp.float32, -lim2, lim2)
        return {'x': x, 'W1': W1, 'b1': b1, 'W2': W2, 'b2': b2}
    _L0_ffn_all = _L0_ffn_setup()
    _L0_ffn_in = {k: v for k, v in _L0_ffn_all.items() if k in ('W1', 'b1', 'W2', 'b2')}
    del _L0_ffn_all
    return {'x': x, 'ctx_1024': ctx_1024, 'mask_BxS2_bk0': mask_BxS2_bk0, 'g_xattn': g_xattn, 'g_ffn': g_ffn, 'L0_xattn_rms_scale': _L0_xattn_in['rms_scale'], 'L0_xattn_q_w': _L0_xattn_in['q_w'], 'L0_xattn_kv_w': _L0_xattn_in['kv_w'], 'L0_xattn_out_w': _L0_xattn_in['out_w'], 'L0_ffn_W1': _L0_ffn_in['W1'], 'L0_ffn_b1': _L0_ffn_in['b1'], 'L0_ffn_W2': _L0_ffn_in['W2'], 'L0_ffn_b2': _L0_ffn_in['b2']}

def reference(x, ctx_1024, mask_BxS2_bk0, g_xattn, g_ffn, L0_xattn_rms_scale, L0_xattn_q_w, L0_xattn_kv_w, L0_xattn_out_w, L0_ffn_W1, L0_ffn_b1, L0_ffn_W2, L0_ffn_b2):
    import jax
    import jax.numpy as jnp

    def _L0_xattn_ref(x, mem_seq, mem_mask, rms_scale, q_w, kv_w, out_w):
        import jax, jax.numpy as jnp
        import numpy as np
        NUM_HEADS, NUM_KV, HEAD_DIM, WIDTH = (4, 1, 64, 256)
        MASK_FILL = -2.3819763e+38

        def _apply_rope(x, positions, max_wavelength=10000.0):
            d = x.shape[-1]
            freq_exp = 2.0 / d * jnp.arange(d // 2, dtype=jnp.float32)
            timescale = max_wavelength ** freq_exp
            radians = positions[..., None].astype(jnp.float32) / timescale
            radians = radians[..., None, :]
            sin, cos = (jnp.sin(radians), jnp.cos(radians))
            x1, x2 = jnp.split(x, 2, axis=-1)
            out = jnp.concatenate([x1 * cos - x2 * sin, x2 * cos + x1 * sin], axis=-1)
            return out.astype(x.dtype)

        def _rmsnorm(x, scale):
            var = jnp.mean(jnp.square(x.astype(jnp.float32)), axis=-1, keepdims=True)
            normed = x * jax.lax.rsqrt(var + 1e-06)
            return (normed * (1 + scale)).astype(x.dtype)
        B, S, _ = mem_seq.shape
        T = x.shape[1]
        G = NUM_HEADS // NUM_KV
        xn = _rmsnorm(x, rms_scale)
        mn = _rmsnorm(mem_seq, rms_scale)
        q = jnp.einsum('BTD,NDH->BTNH', xn, q_w)
        kv = jnp.einsum('BSD,cKDH->cBSKH', mn, kv_w)
        k, v = (kv[0], kv[1])
        q_pos = jnp.broadcast_to(jnp.arange(S, T + S), (B, T))
        k_pos = jnp.broadcast_to(jnp.arange(S), (B, S))
        q = _apply_rope(q, q_pos) * HEAD_DIM ** (-0.5)
        k = _apply_rope(k, k_pos)
        q = q.reshape(B, T, NUM_KV, G, HEAD_DIM)
        logits = jnp.einsum('BTKGH,BSKH->BKGTS', q, k, preferred_element_type=jnp.float32)
        masked = jnp.where(mem_mask[:, None, None, None, :], logits, MASK_FILL)
        probs = jax.nn.softmax(masked, axis=-1).astype(x.dtype)
        enc = jnp.einsum('BKGTS,BSKH->BTKGH', probs, v).reshape(B, T, NUM_HEADS, HEAD_DIM)
        return jnp.einsum('BTNH,NHD->BTD', enc, out_w)

    def _L0_ffn_ref(x, W1, b1, W2, b2):
        import jax, jax.numpy as jnp
        import numpy as np
        EMB = 256
        FF = 4 * EMB

        def _ternary(w):
            scale = jnp.maximum(jnp.mean(jnp.abs(w)), 1e-08)
            w_t = jnp.clip(jnp.round(w / scale), -1.0, 1.0)
            return w + jax.lax.stop_gradient(w_t - w)
        h = jnp.einsum('bsd,fd->bsf', x, _ternary(W1)) + b1
        h = jax.nn.gelu(h, approximate=False)
        out = jnp.einsum('bsf,df->bsd', h, _ternary(W2)) + b2
        return out
    x = x + jnp.tanh(g_xattn[0]) * _L0_xattn_ref(_layernorm(x, axis=-1), ctx_1024, mask_BxS2_bk0, L0_xattn_rms_scale, L0_xattn_q_w, L0_xattn_kv_w, L0_xattn_out_w)
    x = x + jnp.tanh(g_ffn[0]) * _L0_ffn_ref(_layernorm(x, axis=-1), L0_ffn_W1, L0_ffn_b1, L0_ffn_W2, L0_ffn_b2)
    return x

_drawn_inputs = setup_inputs


def setup_inputs(seed=0):
    import zlib

    import numpy as np

    out = dict(_drawn_inputs(seed))
    spreads = {}
    factors = {'L0_xattn_rms_scale': 5.92, 'L0_ffn_b1': 23.71, 'L0_ffn_b2': 64.0}
    for name, (base, spread) in spreads.items():
        noise = np.random.default_rng([zlib.crc32(name.encode()), seed]).standard_normal(out[name].shape)
        drawn = base * np.exp(spread * noise) if base else spread * noise
        out[name] = jnp.asarray(drawn.astype(out[name].dtype))
    for name, factor in factors.items():
        out[name] = (out[name] * factor).astype(out[name].dtype)
    return out
```

```python
from contextlib import ExitStack

import numpy as np

import concourse.bass as bass
from concourse import mybir

F32 = mybir.dt.float32
F32R = mybir.dt.float32r
U8 = mybir.dt.uint8
ALU = mybir.AluOpType
ACT = mybir.ActivationFunctionType
AX = mybir.AxisListType

P = 128
LN_EPS = 1e-5
RMS_EPS = 1e-6
MASK_FILL = -2.3819763e38
MAX_WAVELENGTH = 10000.0



def flamingo_block(nc, x, ctx_main, ctx_tail, mask, gates, rms_scale, wq, wk, wv, wo, w1t, b1, w2t, b2,
                   rope_q_cos, rope_q_sin, rope_k_cos, rope_k_sin, ident, out):
    B, T, D = x.shape
    H = wo.shape[1]
    C = wo.shape[0]
    S = mask.shape[1]
    F = w1t.shape[1]
    KD = D // P
    NT = 4
    GT = NT * P
    NG = B * T // GT
    NF = F // P
    TAIL = S - P
    TP = 32
    HP = H // 2
    CT = B + 1
    assert H * TP == P and B * TP == P and 2 * C == P and NG == 2 * B and KD == 2

    x_g = x.rearrange("b (h t p) d -> (b h) p t d", h=2, t=NT)
    out_g = out.rearrange("b (h t p) d -> (b h) p t d", h=2, t=NT)

    with ExitStack() as ctx:
        def sb(name, shape, dt=F32):
            return ctx.enter_context(nc.sbuf_tensor(name, shape, dt))

        def sem(name):
            return ctx.enter_context(nc.semaphore(name))

        ident_sb = sb("ident_sb", [P, P])
        ones_sb = sb("ones_sb", [P, P])
        neghalf = sb("neghalf", [P, 8])
        gate_raw = sb("gate_raw", [P, 2])
        gate = sb("gate", [P, 2])
        rq_cos = sb("rq_cos", [P, 2 * NT, C // 2])
        rq_sin = sb("rq_sin", [P, 2 * NT, 2, C // 2])
        rk_cos = sb("rk_cos", [P, CT, C // 2])
        rk_sin = sb("rk_sin", [P, CT, 2, C // 2])
        scale_raw = sb("scale_raw", [P, KD])
        scale1 = sb("scale1", [P, KD])
        wq_hi = sb("wq_hi", [P, KD, H * C], F32R)
        wq_lo = sb("wq_lo", [P, KD, H * C], F32R)
        wkv_raw = sb("wkv_raw", [P, KD, 3, C])
        wkv_s = sb("wkv_s", [P, KD, 3, C])
        wo_raw = sb("wo_raw", [P, H, D])
        w_tern = [sb("w1_tern", [P, KD * F], F32R), sb("w2_tern", [P, NF * D], F32R)]
        w_sums = sb("w_sums", [P, 2])
        w_scale = sb("w_scale", [P, 2])
        w_thr = sb("w_thr", [P, 2, 2])
        b1_sb = sb("b1_sb", [P, NF])
        b2_gated = sb("b2_gated", [P, D])
        mask_u8 = sb("mask_u8", [P, B, S], U8)
        mask_bias = sb("mask_bias", [P, B, S])
        mask_now = sb("mask_now", [P, S])
        ctx_bn = sb("ctx_bn", [P, CT, 6])
        ctx_mv = sb("ctx_mv", [P, CT, 2])
        ctx_ms = sb("ctx_ms", [P, CT])
        ctx_m2 = sb("ctx_m2", [P, CT])
        ctx_me = sb("ctx_me", [P, CT])
        ctx_r = sb("ctx_r", [P, CT])
        kk_hi = sb("kk_hi", [P, B, 2 * S], F32R)
        kk_lo = sb("kk_lo", [P, B, 2 * S], F32R)
        vw_hi = sb("vw_hi", [P, B, H + 1, D], F32R)
        vw_lo = sb("vw_lo", [P, B, H + 1, D], F32R)
        x_sb = [sb(f"x_sb{p}", [P, NT, D]) for p in range(2)]
        bn1 = sb("bn1", [P, NT, 6])
        mv1 = sb("mv1", [P, NT, 2])
        ve1 = sb("ve1", [P, NT])
        r1 = sb("r1", [P, NT])
        xn = sb("xn", [P, NT, D])
        xnT_hi = sb("xnT_hi", [P, KD, GT], F32R)
        xnT_lo = sb("xnT_lo", [P, KD, GT], F32R)
        q_cos = [sb(f"q_cos{j}", [P, D]) for j in range(2)]
        q_sin = [sb(f"q_sin{j}", [P, D]) for j in range(2)]
        qT_hi = [sb(f"qT_hi{j}", [P, HP, P], F32R) for j in range(2)]
        qT_lo = [sb(f"qT_lo{j}", [P, HP, P], F32R) for j in range(2)]
        s_neg = [sb(f"s_neg{j}", [P, H, S]) for j in range(2)]
        s_min = [sb(f"s_min{j}", [P, H]) for j in range(2)]
        p_sum = sb("p_sum", [P, NT, H])
        p_inv = sb("p_inv", [P, NT, H])
        pT_hi = [sb(f"pT_hi{j}", [P, H + 1, P], F32R) for j in range(2)]
        pT_lo = [sb(f"pT_lo{j}", [P, H + 1, P], F32R) for j in range(2)]
        bn2 = sb("bn2", [P, NT, 6])
        mv2 = sb("mv2", [P, NT, 2])
        ve2 = sb("ve2", [P, NT])
        r2 = sb("r2", [P, NT])
        x1nT_hi = sb("x1nT_hi", [P, KD, GT], F32R)
        x1nT_lo = sb("x1nT_lo", [P, KD, GT], F32R)

        prob = [sb(f"prob{t}", [P, H, S]) for t in range(NT)]
        prob_tail = sb("prob_tail", [P, NT, H, TP])
        x1_both = sb("x1_both", [P, 2 * NT * D])
        x1 = [x1_both[:, NT * D * p:NT * D * (p + 1)].rearrange("p (t d) -> p t d", t=NT) for p in range(2)]
        x1n = xn
        h_all = sb("h_all", [P, 4 * GT])
        h_act = [h_all[:, GT * j:GT * (j + 1)] for j in range(4)]
        hT_hi = sb("hT_hi", [P, NF, GT], F32R)
        hT_lo = sb("hT_lo", [P, NF, GT], F32R)

        class Borrow:

            def __init__(self, flat):
                self.flat, self.at = flat, 0

            def take(self, n):
                self.at += n
                return self.flat[:, self.at - n:self.at]

        w2_raw = sb("w2_raw", [P, NF * D])
        of_x1, of_w2 = Borrow(x1_both), Borrow(w2_raw)
        of_hi = Borrow(hT_hi[:].rearrange("p c t -> p (c t)"))
        of_lo = Borrow(hT_lo[:].rearrange("p c t -> p (c t)"))
        ctx_flat = of_w2.take(CT * D)
        ctx_sb = ctx_flat.rearrange("p (t d) -> p t d", t=CT)
        ctx_nT = ctx_flat.rearrange("p (k s) -> p k s", k=KD)
        k_rot = of_w2.take(CT * P).rearrange("p (t j c) -> p t j c", t=CT, j=2)
        ctx_n = of_x1.take(CT * D).rearrange("p (t d) -> p t d", t=CT)
        b2_raw = of_x1.take(D)
        k_a, k_b = (s_neg[j][:].rearrange("p h s -> p (h s)")[:, 0:CT * C].rearrange("p (t j c) -> p t j c", t=CT, j=2)
                    for j in range(2))
        wq_s = prob[0][:].rearrange("p h s -> p (h s)")[:, 0:KD * H * C].rearrange("p (k n) -> p k n", k=KD)
        wq_raw = of_x1.take(KD * H * C).rearrange("p (k n) -> p k n", k=KD)
        v_tail = of_hi.take(B * H * P).rearrange("p (b h s) -> p b h s", b=B, h=H)
        v_tmp = of_hi.take(CT * P)
        v_T = of_hi.take(CT * P)
        w_abs = of_lo.take(KD * F)
        wo_hi = of_lo.take(H * D).rearrange("p (h d) -> p h d", h=H)
        wo_lo = of_lo.take(H * D).rearrange("p (h d) -> p h d", h=H)
        w_raw = [h_all, w2_raw]
        w_low = x1_both[:, NT * D:]

        def psum(name):
            return [ctx.enter_context(nc.psum_tensor(f"{name}{j}", [P, 512], F32)) for j in range(2)]

        ps_t, ps_m, ps_s, ps_h = psum("ps_t"), psum("ps_m"), psum("ps_s"), psum("ps_h")

        ctx_in, tab_in, wkv_in, wq_in, wo_in, w_in, gate_in, mask_in, b2_in, ident_in, rope_in = (
            sem(n) for n in ("ctx_in", "tab_in", "wkv_in", "wq_in", "wo_in", "w_in", "gate_in", "mask_in",
                             "b2_in", "ident_in", "rope_in"))
        x_in = [sem("x_in0"), sem("x_in1")]
        out_done = [sem("out_done0"), sem("out_done1")]
        const_set, ctx_zeroed, zeros_set, gate_set = (
            sem(n) for n in ("const_set", "ctx_zeroed", "zeros_set", "gate_set"))
        ctx_bn_done, ctx_stats, ctx_ms_done, ctx_rstd, ctx_normed, ctxT_filled, ctxT_copied = (
            sem(n) for n in ("ctx_bn_done", "ctx_stats", "ctx_ms_done", "ctx_rstd", "ctx_normed",
                             "ctxT_filled", "ctxT_copied"))
        scale1_set, wkv_scaled, wq_scaled, wq_hi_set, wq_set, wo_hi_set, wo_set = (
            sem(n) for n in ("scale1_set", "wkv_scaled", "wq_scaled", "wq_hi_set", "wq_set", "wo_hi_set", "wo_set"))
        k_filled, k_products, k_rotated, kT_filled, kk_hi_set, kk_set = (
            sem(n) for n in ("k_filled", "k_products", "k_rotated", "kT_filled", "kk_hi_set", "kk_set"))
        v_filled, v_hi_set, v_set, v_tail_set, vw_filled, vw_hi_set, vw_set = (
            sem(n) for n in ("v_filled", "v_hi_set", "v_set", "v_tail_set", "vw_filled", "vw_hi_set", "vw_set"))
        w_summed, w_total, w_scaled, w_thr_set, w_low_set, w_set, b2_set, mask_f_set, mask_now_set = (
            sem(n) for n in ("w_summed", "w_total", "w_scaled", "w_thr_set", "w_low_set", "w_set", "b2_set",
                             "mask_f_set", "mask_now_set"))
        t_filled, t_hi, t_lo = sem("t_filled"), sem("t_hi"), sem("t_lo")
        m_filled, m_read = sem("m_filled"), sem("m_read")
        s_filled, s_first, s_masked = sem("s_filled"), sem("s_first"), sem("s_masked")
        h_filled, h_gelu, h_hi, h_split = sem("h_filled"), sem("h_gelu"), sem("h_hi"), sem("h_split")
        bn1_done, ln1_stats, ln1_var, ln1_rstd, xn_done = (
            sem(n) for n in ("bn1_done", "ln1_stats", "ln1_var", "ln1_rstd", "xn_done"))
        bn2_done, ln2_stats, ln2_var, ln2_rstd, x1n_done = (
            sem(n) for n in ("bn2_done", "ln2_stats", "ln2_var", "ln2_rstd", "x1n_done"))
        q_roped, exp_done, inv_done, prob_done, y_base = (
            sem(n) for n in ("q_roped", "exp_done", "inv_done", "prob_done", "y_base"))

        T_SLOT = {"x1n": 0, "q": 2, "p": 6, "xn": 14}

        def t_use(i, kind, k=0):
            if isinstance(i, int) and i == NG:
                return 16 * i - 2 + k
            return i * 16 + (T_SLOT[kind] + k)

        def t_bank(kind, k=0):
            return ps_t[(T_SLOT[kind] + k) % 2]

        M_SLOT = {"q": (0, 1, 4, 6), "y": (2, 3, 5, 7), "att": (8, 9, 10, 11)}

        def m_use(i, kind, t):
            if isinstance(i, int) and i < 2:
                return 8 * i + {"q": 0, "att": 4}[kind] + t
            if isinstance(i, int) and i >= NG:
                return 12 * NG - 8 + 4 * (i - NG) + t
            return i * 12 + (M_SLOT[kind][t] - 8)

        def m_bank(i, kind, t):
            alone = isinstance(i, int) and (i < 2 or i >= NG)
            return ps_m[(t if alone else M_SLOT[kind][t]) % 2]

        def has(i):
            if not isinstance(i, int):
                return True, True, True, True
            return i < NG, i + 1 < NG, 1 <= i <= NG, i >= 2

        def loop(eng, step, between):
            step(0, 0, 0)
            between()
            step(1, 1, 0)
            with eng.Fori(1, B - 1, 1) as b:
                step(b * 2, 0, b)
                step(b * 2 + 1, 1, b)
            for i in range(NG - 2, NG + 2):
                step(i, i % 2, i // 2)

        VW = [(b, h) for b in range(B) for h in (0, 2, None)]
        vw_banks = [ps_h[0], ps_h[1], ps_s[0], ps_s[1]]

        def vw_slot(dst, b, h):
            if h is None:
                return dst[:, b, H, :], slice(0, D)
            return dst[:, b, h:h + 2, :].rearrange("p a d -> p (a d)"), slice(0, 2 * D)

        def kk_parts(dst, rows, col):
            main = ps_s[0][rows, :].rearrange("p (b s) -> p b s", b=B)
            tails = ps_s[1][rows, 0:P].rearrange("p (b s) -> p b s", b=B)[:, :, 0:TAIL]
            return [(dst[rows, :, col:col + P], main), (dst[rows, :, col + P:col + S], tails)]

        block = ctx.enter_context(nc.Block())

        @block.sync
        def _(sp):
            sp.dma_start(ctx_sb[:, 0:B, :], ctx_main.rearrange("b p d -> p b d")).then_inc(ctx_in, 16)
            sp.wait_ge(ctx_zeroed, 1)
            for b in range(B):
                sp.dma_start(ctx_sb[TP * b:TP * b + TAIL, B, :], ctx_tail[b]).then_inc(ctx_in, 16)
            sp.dma_start(x_sb[0][:], x_g[0]).then_inc(x_in[0], 16)
            sp.dma_start(rq_cos[:], rope_q_cos).then_inc(rope_in, 16)
            sp.dma_start(rq_sin[:], rope_q_sin).then_inc(rope_in, 16)
            sp.dma_start(x_sb[1][:], x_g[1]).then_inc(x_in[1], 16)
            sp.dma_start(b1_sb[:], b1).then_inc(w_in, 16)
            sp.dma_start(w_raw[0][:].rearrange("p (k f) -> p k f", k=KD),
                         w1t.rearrange("(k p) f -> p k f", p=P)).then_inc(w_in, 16)
            sp.wait_ge(v_filled, 2)
            sp.wait_ge(kT_filled, 2)
            sp.dma_start(w_raw[1][:].rearrange("p (k f) -> p k f", k=NF),
                         w2t.rearrange("(k p) d -> p k d", p=P)).then_inc(w_in, 16)

            def step(i, p, b):
                att, _, _, y = has(i)
                if y:
                    sp.wait_ge(m_read, m_use(i, "y", NT - 1) + 1)
                    sp.dma_start(out_g[i - 2], x1[p][:]).then_inc(out_done[p], 16)
                if att and not (isinstance(i, int) and i + 2 >= NG):
                    sp.wait_ge(bn2_done, i * NT + NT)
                    sp.dma_start(x_sb[p][:], x_g[i + 2]).then_inc(x_in[p], 16)

            loop(sp, step, lambda: None)
            for p in range(2):
                sp.wait_ge(out_done[p], 16 * B)

        @block.gpsimd
        def _(pool):
            pool.memset(ctx_sb[:, B, :], 0.0).then_inc(ctx_zeroed, 1)
            pool.memset(neghalf[:], -0.5).then_inc(const_set, 1)
            pool.memset(ones_sb[:], 1.0).then_inc(const_set, 1)
            pool.dma_start(gate_raw[:, :], gates.partition_broadcast(P)).then_inc(gate_in, 16)
            pool.dma_start(mask_u8[:], mask.partition_broadcast(P)).then_inc(mask_in, 16)
            pool.dma_start(b2_raw, b2.partition_broadcast(P)).then_inc(b2_in, 16)

            pool.wait_ge(ctx_stats, 1)
            pool.tensor_tensor(ctx_m2[:], ctx_mv[:, :, 0], ctx_mv[:, :, 0], ALU.mult).then_inc(ctx_ms_done, 1)
            pool.wait_ge(ctx_ms_done, 1)
            pool.tensor_tensor(ctx_ms[:], ctx_m2[:], ctx_mv[:, :, 1], ALU.add).then_inc(ctx_ms_done, 1)
            pool.wait_ge(ctx_ms_done, 2)
            pool.tensor_scalar(ctx_me[:], ctx_ms[:], RMS_EPS, None, ALU.add).then_inc(ctx_ms_done, 1)
            pool.wait_ge(ctx_ms_done, 3)
            pool.wait_ge(const_set, 1)
            pool.tensor_tensor(ctx_r[:], ctx_me[:], neghalf[:, 0:CT], ALU.pow).then_inc(ctx_rstd, 1)

            def rstd(ve, r, var_sem, rstd_sem, i):
                pool.wait_ge(var_sem, i + 1)
                pool.tensor_tensor(r[:], ve[:], neghalf[:, 0:NT], ALU.pow).then_inc(rstd_sem, 1)

            rstd(ve1, r1, ln1_var, ln1_rstd, 0)
            pool.memset(prob_tail[:], 0.0).then_inc(zeros_set, 1)
            pool.memset(kk_hi[:].bitcast(F32), 0.0).then_inc(zeros_set, 1)
            pool.memset(kk_lo[:].bitcast(F32), 0.0).then_inc(zeros_set, 1)
            pool.memset(v_tail.bitcast(F32), 0.0).then_inc(zeros_set, 1)
            pool.wait_ge(wo_hi_set, 1)
            pool.tensor_tensor(wo_lo[:], wo_raw[:], wo_hi[:], ALU.subtract).then_inc(wo_set, 1)
            pool.wait_ge(v_set, 2)
            pool.wait_ge(zeros_set, 4)
            for h in range(H):
                pool.tensor_copy(v_tail[:, :, h, TP * h:TP * (h + 1)],
                                 v_T[:, B * P:].rearrange("p (b j) -> p b j", b=B)).then_inc(v_tail_set, 1)

            def step(i, p, b):
                att, nxt, f1, _ = has(i)

                def add_b2():
                    if f1:
                        pool.wait_ge(x1n_done, i * NT)
                        if isinstance(i, int) and i == 1:
                            pool.wait_ge(b2_set, 1)
                        b2s = b2_gated[:].rearrange("p (a d) -> p a d", a=1).to_broadcast([P, NT, D])
                        pool.tensor_tensor(x1[1 - p], x1[1 - p], b2s, ALU.add).then_inc(y_base, 1)

                if not att:
                    add_b2()
                    return

                def rope_add(t):
                    pool.wait_ge(m_read, m_use(i, "q", t) + 1)
                    q = q_cos[t % 2]
                    pool.tensor_tensor(q[:], q[:], q_sin[t % 2][:], ALU.add).then_inc(q_roped, 1)

                def normalise(t):
                    pool.wait_ge(inv_done, i * NT + (t + 1))
                    inv = p_inv[:, t, :].rearrange("p (h a) -> p h a", a=1)
                    main, tail = prob[t][:, :, 0:P], prob[t][:, :, P:S]
                    pool.tensor_tensor(main, main, inv.to_broadcast([P, H, P]), ALU.mult)
                    pool.tensor_tensor(prob_tail[:, t, :, 0:TAIL], tail, inv.to_broadcast([P, H, TAIL]),
                                       ALU.mult).then_inc(prob_done, 1)

                rope_add(0)
                rope_add(1)
                rope_add(2)
                normalise(0)
                rope_add(3)
                add_b2()
                normalise(1)
                normalise(2)
                if nxt:
                    rstd(ve1, r1, ln1_var, ln1_rstd, i + 1)
                normalise(3)
                rstd(ve2, r2, ln2_var, ln2_rstd, i)

            loop(pool, step, lambda: None)

        @block.scalar
        def _(act):
            act.dma_start(ident_sb[:], ident).then_inc(ident_in, 16)
            act.dma_start(scale_raw[:], rms_scale).then_inc(wkv_in, 16)
            act.dma_start(wkv_raw[:, :, 0, :], wk.rearrange("(k p) c -> p k c", p=P)).then_inc(wkv_in, 16)
            for j in (1, 2):
                act.dma_start(wkv_raw[:, :, j, :], wv.rearrange("(k p) c -> p k c", p=P)).then_inc(wkv_in, 16)
            act.dma_start(wq_raw[:], wq.rearrange("(k p) n -> p k n", p=P)).then_inc(wq_in, 16)
            act.dma_start(rk_cos[:], rope_k_cos).then_inc(tab_in, 16)
            act.dma_start(rk_sin[:], rope_k_sin).then_inc(tab_in, 16)
            for r in (0, C):
                act.dma_start(wo_raw[r:r + C], wo).then_inc(wo_in, 16)
            act.wait_ge(gate_in, 16)
            nc.scalar.activation(gate[:], gate_raw[:], ACT.Tanh).then_inc(gate_set, 1)
            act.wait_ge(wo_in, 32)
            nc.scalar.activation(wo_hi[:], wo_raw[:], ACT.Copy).then_inc(wo_hi_set, 1)
            for k in range(KD):
                act.wait_ge(ctxT_filled, k + 1)
                nc.scalar.activation(ctx_nT[:, k, 0:B * P], ps_s[k][:], ACT.Copy).then_inc(ctxT_copied, 1)
            act.wait_ge(ctxT_filled, 3)
            nc.scalar.activation(ctx_nT[:, :, B * P:], ps_h[0][:, 0:KD * P].rearrange("p (k s) -> p k s", k=KD),
                                 ACT.Copy).then_inc(ctxT_copied, 1)

            def hi_part(n, dst, src):
                act.wait_ge(t_filled, n + 1)
                nc.scalar.activation(dst, src, ACT.Copy).then_inc(t_hi, 1)

            for k in range(KD):
                hi_part(k, xnT_hi[:, k, :], t_bank("xn", k)[:])
            for n, (cols, ps) in enumerate(((slice(0, B * P), ps_m[0][:]), (slice(B * P, CT * P), ps_m[1][:, 0:P]))):
                act.wait_ge(v_filled, n + 1)
                nc.scalar.activation(v_T[0:C, cols], ps[0:C], ACT.Copy).then_inc(v_hi_set, 1)
                nc.scalar.activation(v_tmp[C:P, cols], ps[C:P], ACT.Copy).then_inc(v_hi_set, 1)
            act.wait_ge(kT_filled, 2)
            act.wait_ge(zeros_set, 3)
            for half in range(2):
                rows = slice(C * half, C * (half + 1))
                for dst, src in kk_parts(kk_hi, rows, S * half):
                    nc.scalar.activation(dst, src, ACT.Copy).then_inc(kk_hi_set, 1)
            for n, (b, h) in enumerate(VW):
                act.wait_ge(vw_filled, n + 1)
                dst, cols = vw_slot(vw_hi, b, h)
                nc.scalar.activation(dst, vw_banks[n % 4][:, cols], ACT.Copy, scale=gate[:, 0:1]).then_inc(vw_hi_set, 1)
            act.wait_ge(w_in, 16 * 3)
            for m in range(2):
                if m:
                    act.wait_ge(w_summed, m)
                nc.scalar.activation(w_abs[:], w_raw[m][:, :], ACT.Abs, accum_out=w_sums[:, m:m + 1]).then_inc(w_summed, 1)

            def step(i, p, b):
                att, nxt, f1, _ = has(i)

                def q_hi(t):
                    hi_part(t_use(i, "q", t), qT_hi[t % 2][:].rearrange("p a b -> p (a b)"), t_bank("q", t)[:, 0:D])

                def exps(t):
                    act.wait_ge(s_masked, i * NT + (t + 1))
                    for h in range(H):
                        e = nc.scalar.activation(prob[t][:, h, :], s_neg[t % 2][:, h, :], ACT.Exp,
                                                 bias=s_min[t % 2][:, h:h + 1], scale=-1.0,
                                                 accum_out=p_sum[:, t, h:h + 1])
                    e.then_inc(exp_done, 1)

                def p_hi(t):
                    if t < 2:
                        if not (isinstance(i, int) and i == 0):
                            act.wait_ge(m_filled, m_use(i - 1, "att", t + 2) + 1)
                    else:
                        act.wait_ge(m_filled, m_use(i, "att", t - 2) + 1)
                    hi_part(t_use(i, "p", 2 * t), pT_hi[t % 2][:, 0:H, :].rearrange("p h s -> p (h s)"),
                            t_bank("p", 2 * t)[:])
                    hi_part(t_use(i, "p", 2 * t + 1), pT_hi[t % 2][:, H, :], t_bank("p", 2 * t + 1)[:, 0:P])

                def gelu(c):
                    if not f1:
                        return
                    act.wait_ge(h_filled, i * NF + (c + 1 - NF))
                    if not (isinstance(i, int) and i == 1 and c < 4):
                        act.wait_ge(h_split, i * NF + (c - 3 - NF))
                    nc.scalar.activation(h_act[c % 4][:], ps_h[c % 2][:], ACT.Gelu,
                                         bias=b1_sb[:, c:c + 1]).then_inc(h_gelu, 1)

                if f1:
                    for k in range(KD):
                        hi_part(t_use(i, "x1n", k), x1nT_hi[:, k, :], t_bank("x1n", k)[:])
                if att:
                    q_hi(0)
                    q_hi(1)
                    exps(0)
                    q_hi(2)
                    exps(1)
                    q_hi(3)
                    exps(2)
                    p_hi(0)
                    exps(3)
                gelu(0)
                if att:
                    p_hi(1)
                gelu(1)
                if att:
                    p_hi(2)
                gelu(2)
                if att:
                    p_hi(3)
                gelu(3)
                gelu(4)
                gelu(5)
                if nxt:
                    for k in range(KD):
                        hi_part(t_use(i, "xn", k), xnT_hi[:, k, :], t_bank("xn", k)[:])
                gelu(6)
                gelu(7)

            loop(act, step, lambda: None)

        @block.vector
        def _(dve):
            dve.wait_ge(ctx_in, 16 * (B + 1))
            for t in range(CT):
                dve.bn_stats(ctx_bn[:, t, :], ctx_sb[:, t, :]).then_inc(ctx_bn_done, 1)
            dve.wait_ge(ctx_bn_done, CT)
            for t in range(CT):
                s = dve.bn_aggr(ctx_mv[:, t, :], ctx_bn[:, t, :])
            s.then_inc(ctx_stats, 1)

            def sums1(i, p, b):
                dve.wait_ge(x_in[p], b * 16 + 16)
                for t in range(NT):
                    dve.bn_stats(bn1[:, t, :], x_sb[p][:, t, :]).then_inc(bn1_done, 1)

            def variances(i, bn, mv, stats_sem, ve, var_sem, mul, add):
                for t in range(NT):
                    s = dve.bn_aggr(mv[:, t, :], bn[:, t, :])
                s.then_inc(stats_sem, 1)
                dve.wait_ge(stats_sem, i + 1)
                dve.tensor_scalar(ve[:], mv[:, :, 1], mul, add, ALU.mult, ALU.add).then_inc(var_sem, 1)

            def variances1(i):
                variances(i, bn1, mv1, ln1_stats, ve1, ln1_var, 1.0 + RMS_EPS, LN_EPS * RMS_EPS)

            def variances2(i):
                variances(i, bn2, mv2, ln2_stats, ve2, ln2_var, 1.0, LN_EPS)

            def norm1(i, p):
                dve.wait_ge(ln1_rstd, i + 1)
                for t in range(NT):
                    dve.tensor_scalar(xn[:, t, :], x_sb[p][:, t, :], mv1[:, t, 0:1], r1[:, t:t + 1],
                                      ALU.subtract, ALU.mult).then_inc(xn_done, 1)

            def lo_part(n, dst, src, hi):
                dve.wait_ge(t_hi, n + 1)
                dve.tensor_tensor(dst, src, hi, ALU.subtract).then_inc(t_lo, 1)

            dve.wait_ge(wkv_in, 16 * 4)
            dve.tensor_scalar(scale1[:], scale_raw[:], 1.0, None, ALU.add).then_inc(scale1_set, 1)
            dve.wait_ge(scale1_set, 1)
            for k in range(KD):
                dve.tensor_scalar(wkv_s[:, k], wkv_raw[:, k], scale1[:, k:k + 1], None, ALU.mult).then_inc(wkv_scaled, 1)
            dve.wait_ge(ctx_rstd, 1)
            for t in range(CT):
                dve.tensor_scalar(ctx_n[:, t, :], ctx_sb[:, t, :], ctx_r[:, t:t + 1], None,
                                  ALU.mult).then_inc(ctx_normed, 1)
            sums1(0, 0, 0)
            dve.wait_ge(bn1_done, NT)
            variances1(0)
            dve.wait_ge(wq_in, 16)
            for k in range(KD):
                dve.tensor_scalar(wq_s[:, k], wq_raw[:, k], scale1[:, k:k + 1], None, ALU.mult).then_inc(wq_scaled, 1)
            dve.wait_ge(wq_scaled, KD)
            dve.tensor_copy(wq_hi[:], wq_s).then_inc(wq_hi_set, 1)
            dve.wait_ge(wq_hi_set, 1)
            dve.tensor_tensor(wq_lo[:], wq_s, wq_hi[:], ALU.subtract).then_inc(wq_set, 1)
            norm1(0, 0)
            dve.wait_ge(k_filled, 1)
            dve.wait_ge(tab_in, 32)
            kps = ps_h[1][:, 0:CT * C].rearrange("p (t j c) -> p t j c", t=CT, j=2)
            for j in range(2):
                dve.tensor_tensor(k_a[:, :, j, :], kps[:, :, j, :], rk_cos[:], ALU.mult).then_inc(k_products, 1)
                dve.tensor_tensor(k_b[:, :, 1 - j, :], kps[:, :, j, :], rk_sin[:, :, j, :],
                                  ALU.mult).then_inc(k_products, 1)
            dve.wait_ge(k_products, 4)
            for j in range(2):
                dve.tensor_tensor(k_rot[:, :, j, :], k_a[:].rearrange("p t j c -> p t (j c)"),
                                  k_b[:].rearrange("p t j c -> p t (j c)"), ALU.add).then_inc(k_rotated, 1)
            for k in range(KD):
                lo_part(k, xnT_lo[:, k, :], t_bank("xn", k)[:], xnT_hi[:, k, :])
            for n, (cols, ps) in enumerate(((slice(0, B * P), ps_m[0][:]), (slice(B * P, CT * P), ps_m[1][:, 0:P]))):
                dve.wait_ge(v_hi_set, 2 * n + 2)
                dve.tensor_tensor(v_T[C:P, cols], ps[C:P], v_tmp[C:P, cols], ALU.subtract).then_inc(v_set, 1)
            dve.wait_ge(kk_hi_set, 4)
            for half in range(2):
                rows = slice(C * half, C * (half + 1))
                for (dst, src), (hi, _) in zip(kk_parts(kk_lo, rows, S * half), kk_parts(kk_hi, rows, S * half)):
                    dve.tensor_tensor(dst, src, hi, ALU.subtract).then_inc(kk_set, 1)
            dve.wait_ge(mask_in, 16)
            dve.tensor_scalar(mask_bias[:], mask_u8[:], MASK_FILL, -MASK_FILL, ALU.mult, ALU.add).then_inc(mask_f_set, 1)
            dve.wait_ge(gate_set, 1)
            dve.wait_ge(b2_in, 16)
            dve.tensor_scalar(b2_gated[:], b2_raw, gate[:, 1:2], None, ALU.mult).then_inc(b2_set, 1)
            for n, (b, h) in enumerate(VW):
                dve.wait_ge(vw_hi_set, n + 1)
                hi, cols = vw_slot(vw_hi, b, h)
                dve.scalar_tensor_tensor(vw_slot(vw_lo, b, h)[0], vw_banks[n % 4][:, cols], gate[:, 0:1], hi,
                                         ALU.mult, ALU.subtract).then_inc(vw_set, 1)
            dve.wait_ge(mask_f_set, 1)
            dve.wait_ge(rope_in, 32)

            def ternary():
                dve.wait_ge(w_total, 1)
                dve.tensor_scalar(w_scale[:], ps_h[0][:, 0:2], 1.0 / (D * F), 1e-8, ALU.mult,
                                  ALU.max).then_inc(w_scaled, 1)
                dve.wait_ge(w_scaled, 1)
                for n, sign in enumerate((0.5, -0.5)):
                    dve.tensor_scalar(w_thr[:, n, :], w_scale[:], sign, None, ALU.mult).then_inc(w_thr_set, 1)
                dve.wait_ge(w_thr_set, 2)
                for n in range(4):
                    m, cols = n // 2, slice(n % 2 * NT * D, (n % 2 + 1) * NT * D)
                    if n:
                        dve.wait_ge(w_set, n)
                    dve.tensor_scalar(w_low, w_raw[m][:, cols], w_thr[:, 1, m:m + 1], None,
                                      ALU.is_lt).then_inc(w_low_set, 1)
                    dve.wait_ge(w_low_set, n + 1)
                    dve.scalar_tensor_tensor(w_tern[m][:, cols], w_raw[m][:, cols], w_thr[:, 0, m:m + 1], w_low,
                                             ALU.is_gt, ALU.subtract).then_inc(w_set, 1)

            def step(i, p, b):
                att, nxt, f1, y = has(i)
                first = isinstance(i, int) and i == 0

                def rope(t):
                    n = m_use(i, "q", t)
                    dve.wait_ge(m_filled, n + 1)
                    q = m_bank(i, "q", t)[:, 0:D]
                    pos = NT * p + t
                    cos = rq_cos[:, pos, :].rearrange("p (a c) -> p a c", a=1).to_broadcast([P, 2 * H, C // 2])
                    dve.tensor_tensor(q_cos[t % 2][:].rearrange("p (a c) -> p a c", a=2 * H),
                                      q.rearrange("p (a c) -> p a c", a=2 * H), cos, ALU.mult)
                    sin = rq_sin[:, pos].rearrange("p (a j) c -> p a j c", a=1).to_broadcast([P, H, 2, C // 2])
                    dve.tensor_tensor(q_sin[t % 2][:].rearrange("p (h j c) -> p h j c", h=H, j=2)[:, :, ::-1, :],
                                      q.rearrange("p (h j c) -> p h j c", h=H, j=2), sin,
                                      ALU.mult).then_inc(m_read, 1)

                def q_lo(t):
                    lo_part(t_use(i, "q", t), qT_lo[t % 2][:].rearrange("p a b -> p (a b)"),
                            t_bank("q", t)[:, 0:D], qT_hi[t % 2][:].rearrange("p a b -> p (a b)"))

                def mask_and_min(t):
                    dve.wait_ge(s_filled, i * NT + (t + 1))
                    s, least = s_neg[t % 2], s_min[t % 2]
                    dve.tensor_tensor(s[:, 0, :], ps_s[0][:, 0:S], mask_now[:], ALU.add).then_inc(s_first, 1)
                    for h in range(1, H):
                        dve.tensor_tensor_reduce(
                            s[:, h, :], ps_s[h // 2][:, S * (h % 2):S * (h % 2 + 1)], mask_now[:],
                            1.0, 3.4e38, ALU.add, ALU.min, least[:, h:h + 1])
                    dve.wait_ge(s_first, i * NT + (t + 1))
                    dve.tensor_reduce(least[:, 0:1], s[:, 0, :], AX.X, ALU.min).then_inc(s_masked, 1)

                def inverse(t):
                    dve.wait_ge(exp_done, i * NT + (t + 1))
                    dve.reciprocal(p_inv[:, t, :], p_sum[:, t, :]).then_inc(inv_done, 1)

                def ffn_out(t):
                    if not y:
                        return
                    n = m_use(i, "y", t)
                    dve.wait_ge(m_filled, n + 1)
                    dve.wait_ge(y_base, i - 1)
                    ys = x1[p][:, t, :]
                    dve.scalar_tensor_tensor(ys, m_bank(i, "y", t)[:, 0:D], gate[:, 1:2], ys,
                                             ALU.mult, ALU.add).then_inc(m_read, 1)

                def p_lo(t):
                    lo_part(t_use(i, "p", 2 * t), pT_lo[t % 2][:, 0:H, :].rearrange("p h s -> p (h s)"),
                            t_bank("p", 2 * t)[:], pT_hi[t % 2][:, 0:H, :].rearrange("p h s -> p (h s)"))
                    lo_part(t_use(i, "p", 2 * t + 1), pT_lo[t % 2][:, H, :], t_bank("p", 2 * t + 1)[:, 0:P],
                            pT_hi[t % 2][:, H, :])

                def residual(t):
                    n = m_use(i, "att", t)
                    dve.wait_ge(m_filled, n + 1)
                    if t == 0 and not (isinstance(i, int) and i < 2):
                        dve.wait_ge(out_done[p], b * 16)
                    dve.tensor_tensor(x1[p][:, t, :], m_bank(i, "att", t)[:, 0:D], x_sb[p][:, t, :],
                                      ALU.add).then_inc(m_read, 1)
                    dve.wait_ge(m_read, n + 1)
                    dve.bn_stats(bn2[:, t, :], x1[p][:, t, :]).then_inc(bn2_done, 1)

                def split_h(c):
                    if not f1:
                        return
                    g = i * NF + (c + 1 - NF)
                    dve.wait_ge(h_gelu, g)
                    dve.tensor_copy(hT_hi[:, c, :], h_act[c % 4][:]).then_inc(h_hi, 1)
                    dve.wait_ge(h_hi, g)
                    dve.tensor_tensor(hT_lo[:, c, :], h_act[c % 4][:], hT_hi[:, c, :], ALU.subtract).then_inc(h_split, 1)

                if att:
                    if p == 0:
                        dve.tensor_copy(mask_now[:], mask_bias[:, b, :]).then_inc(mask_now_set, 1)
                    rope(0)
                    rope(1)
                if f1:
                    for k in range(KD):
                        lo_part(t_use(i, "x1n", k), x1nT_lo[:, k, :], t_bank("x1n", k)[:], x1nT_hi[:, k, :])
                ffn_out(0)
                if att:
                    q_lo(0)
                    if p == 0:
                        dve.wait_ge(mask_now_set, b + 1)
                ffn_out(1)
                if att:
                    q_lo(1)
                    mask_and_min(0)
                    rope(2)
                ffn_out(2)
                if att:
                    q_lo(2)
                    mask_and_min(1)
                    inverse(0)
                    rope(3)
                ffn_out(3)
                if att:
                    q_lo(3)
                    mask_and_min(2)
                    inverse(1)
                    mask_and_min(3)
                    inverse(2)
                if nxt:
                    sums1(i + 1, 1 - p, b if p == 0 else b + 1)
                    dve.wait_ge(bn1_done, i * NT + 2 * NT)
                if att:
                    p_lo(0)
                    if nxt:
                        variances1(i + 1)
                    inverse(3)
                split_h(0)
                if att:
                    residual(0)
                    p_lo(1)
                if nxt:
                    norm1(i + 1, 1 - p)
                split_h(1)
                if att:
                    residual(1)
                    p_lo(2)
                split_h(2)
                if att:
                    residual(2)
                    p_lo(3)
                split_h(3)
                split_h(4)
                if att:
                    residual(3)
                    dve.wait_ge(bn2_done, i * NT + NT)
                split_h(5)
                if att:
                    variances2(i)
                if nxt:
                    for k in range(KD):
                        lo_part(t_use(i, "xn", k), xnT_lo[:, k, :], t_bank("xn", k)[:], xnT_hi[:, k, :])
                split_h(6)
                if att:
                    dve.wait_ge(ln2_rstd, i + 1)
                    for t in range(NT):
                        dve.tensor_scalar(x1n[:, t, :], x1[p][:, t, :], mv2[:, t, 0:1], r2[:, t:t + 1],
                                          ALU.subtract, ALU.mult).then_inc(x1n_done, 1)
                split_h(7)

            loop(dve, step, ternary)

        @block.tensor
        def _(pe):
            def products(dst, pairs):
                for n, (lhs, rhs) in enumerate(pairs):
                    m = pe.matmul(dst, lhs, rhs, start=(n == 0), stop=(n == len(pairs) - 1))
                return m

            def transposed_tiles(n, dst, src, k):
                if not (isinstance(n, int) and n < 2):
                    pe.wait_ge(t_lo, n - 1)
                for t in range(NT):
                    m = pe.transpose(dst[:, P * t:P * (t + 1)], src[:, t, P * k:P * (k + 1)], ident_sb[:])
                m.then_inc(t_filled, 1)

            pe.wait_ge(ident_in, 16)
            pe.wait_ge(ctx_normed, CT)
            for k in range(KD):
                for t in range(B):
                    m = pe.transpose(ps_s[k][:, P * t:P * (t + 1)], ctx_n[:, t, P * k:P * (k + 1)], ident_sb[:])
                m.then_inc(ctxT_filled, 1)
            for k in range(KD):
                m = pe.transpose(ps_h[0][:, P * k:P * (k + 1)], ctx_n[:, B, P * k:P * (k + 1)], ident_sb[:])
            m.then_inc(ctxT_filled, 1)
            pe.wait_ge(xn_done, NT)
            for k in range(KD):
                transposed_tiles(k, t_bank("xn", k), xn, k)
            pe.wait_ge(wkv_scaled, KD)
            pe.wait_ge(ctxT_copied, 3)
            for t in range(CT):
                m = products(ps_h[1][:, C * t:C * (t + 1)],
                             [(ctx_nT[:, k, P * t:P * (t + 1)], wkv_s[:, k, 0, :]) for k in range(KD)])
            m.then_inc(k_filled, 1)
            for cols, dst in ((slice(0, B * P), ps_m[0][:]), (slice(B * P, CT * P), ps_m[1][:, 0:P])):
                products(dst, [(wkv_s[:, k, 1:3, :].rearrange("p a c -> p (a c)"), ctx_nT[:, k, cols])
                               for k in range(KD)]).then_inc(v_filled, 1)
            pe.wait_ge(k_rotated, 2)
            for t in range(CT):
                dst = ps_s[0][:, P * t:P * (t + 1)] if t < B else ps_s[1][:, 0:P]
                m = pe.transpose(dst, k_rot[:, t].rearrange("p j c -> p (j c)"), ident_sb[:])
                if t >= B - 1:
                    m.then_inc(kT_filled, 1)
            pe.wait_ge(v_set, 2)
            pe.wait_ge(wo_set, 1)
            for n, (b, h) in enumerate(VW):
                if n == 2:
                    pe.wait_ge(v_tail_set, H)
                    pe.wait_ge(kk_set, 4)
                if n >= 4:
                    pe.wait_ge(vw_set, n - 3)
                if h is None:
                    pairs = [(v_tail[:, b, j, :], w[:, j, :]) for w in (wo_hi, wo_lo) for j in range(H)]
                else:
                    pairs = [(v_T[:, P * b:P * (b + 1)], w[:, h:h + 2, :].rearrange("p a d -> p (a d)"))
                             for w in (wo_hi, wo_lo)]
                products(vw_banks[n % 4][:, vw_slot(vw_hi, b, h)[1]], pairs).then_inc(vw_filled, 1)
            pe.wait_ge(wq_set, 1)
            pe.wait_ge(vw_set, len(VW))

            def sum_weights():
                pe.wait_ge(w_summed, 2)
                pe.wait_ge(const_set, 2)
                pe.matmul(ps_h[0][:, 0:2], ones_sb[:], w_sums[:], start=True, stop=True).then_inc(w_total, 1)

            def step(i, p, b):
                att, nxt, f1, y = has(i)

                def bank_m(kind, t):
                    n = m_use(i, kind, t)
                    if not (isinstance(n, int) and n < 2):
                        pe.wait_ge(m_read, n - 1)
                    return m_bank(i, kind, t)[:, 0:D]

                def q(t):
                    if not att:
                        return
                    if t == 0:
                        pe.wait_ge(t_lo, xn_ready)
                    tile = slice(P * t, P * (t + 1))
                    dst = bank_m("q", t)
                    products(dst, [(a[:, k, tile], w[:, k, :]) for k in range(KD)
                                   for a, w in ((xnT_hi, wq_hi), (xnT_hi, wq_lo), (xnT_lo, wq_hi))]
                             ).then_inc(m_filled, 1)

                def q_T(t):
                    if not att:
                        return
                    n = t_use(i, "q", t)
                    pe.wait_ge(t_lo, n - 1)
                    pe.wait_ge(q_roped, i * NT + (t + 1))
                    for a in range(HP):
                        m = pe.transpose(t_bank("q", t)[:, P * a:P * (a + 1)], q_cos[t % 2][:, P * a:P * (a + 1)],
                                         ident_sb[:])
                    m.then_inc(t_filled, 1)

                def scores(t):
                    if not att:
                        return
                    pe.wait_ge(t_lo, t_use(i, "q", t) + 1)
                    if not (isinstance(i, int) and i == 0 and t == 0):
                        pe.wait_ge(s_masked, i * NT + t)
                    for a in range(HP):
                        m = products(ps_s[a][:, 0:2 * S],
                                     [(qT_hi[t % 2][:, a, :], kk_hi[:, b, :]), (qT_hi[t % 2][:, a, :], kk_lo[:, b, :]),
                                      (qT_lo[t % 2][:, a, :], kk_hi[:, b, :])])
                    m.then_inc(s_filled, 1)

                def p_T(t):
                    if not att:
                        return
                    pe.wait_ge(prob_done, i * NT + (t + 1))
                    n = t_use(i, "p", 2 * t)
                    pe.wait_ge(t_lo, n - 1)
                    for h in range(H):
                        m = pe.transpose(t_bank("p", 2 * t)[:, P * h:P * (h + 1)], prob[t][:, h, 0:P], ident_sb[:])
                    m.then_inc(t_filled, 1)
                    pe.wait_ge(t_lo, n)
                    pe.transpose(t_bank("p", 2 * t + 1)[:, 0:P], prob_tail[:, t].rearrange("p h s -> p (h s)"), ident_sb[:]).then_inc(t_filled, 1)

                def attend(t):
                    if not att:
                        return
                    pe.wait_ge(t_lo, t_use(i, "p", 2 * t + 1) + 1)
                    dst = bank_m("att", t)
                    hi, lo = pT_hi[t % 2], pT_lo[t % 2]
                    products(dst, [(a[:, c, :], w[:, b, c, :]) for c in range(H + 1)
                                   for a, w in ((hi, vw_hi), (hi, vw_lo), (lo, vw_hi))]).then_inc(m_filled, 1)

                def x1_T():
                    if f1:
                        pe.wait_ge(x1n_done, i * NT)
                        for k in range(KD):
                            transposed_tiles(t_use(i, "x1n", k), t_bank("x1n", k), x1n, k)

                def ffn_in(c):
                    if not f1:
                        return
                    if c == 0:
                        pe.wait_ge(t_lo, t_use(i, "x1n", 1) + 1)
                        if isinstance(i, int) and i == 1:
                            pe.wait_ge(w_set, 4)
                    if not (isinstance(i, int) and i == 1 and c < 2):
                        pe.wait_ge(h_gelu, i * NF + (c - 1 - NF))
                    w = w_tern[0][:].rearrange("p (k f) -> p k f", k=KD)
                    products(ps_h[c % 2][:], [(w[:, k, P * c:P * (c + 1)], a[:, k, :]) for k in range(KD)
                                              for a in (x1nT_hi, x1nT_lo)]).then_inc(h_filled, 1)

                def ffn_out(t):
                    if not y:
                        return
                    if t == 0:
                        pe.wait_ge(h_split, i * NF - NF)
                    w = w_tern[1][:].rearrange("p (c d) -> p c d", c=NF)
                    dst = bank_m("y", t)
                    products(dst, [(a[:, c, P * t:P * (t + 1)], w[:, c, :]) for c in range(NF)
                                   for a in (hT_hi, hT_lo)]).then_inc(m_filled, 1)

                xn_ready = 2 if isinstance(i, int) and i == 0 else i * 16
                q(0)
                q(1)
                x1_T()
                ffn_out(0)
                q_T(0)
                ffn_out(1)
                q_T(1)
                scores(0)
                q(2)
                ffn_out(2)
                q_T(2)
                scores(1)
                q(3)
                ffn_out(3)
                q_T(3)
                scores(2)
                scores(3)
                p_T(0)
                ffn_in(0)
                attend(0)
                p_T(1)
                ffn_in(1)
                attend(1)
                p_T(2)
                ffn_in(2)
                attend(2)
                p_T(3)
                ffn_in(3)
                ffn_in(4)
                attend(3)
                ffn_in(5)
                if nxt:
                    pe.wait_ge(xn_done, i * NT + 2 * NT)
                    for k in range(KD):
                        transposed_tiles(t_use(i, "xn", k), t_bank("xn", k), xn, k)
                ffn_in(6)
                ffn_in(7)

            loop(pe, step, sum_weights)


def _rotation(positions, half):
    timescale = np.float32(MAX_WAVELENGTH) ** (np.float32(1.0 / half) * np.arange(half, dtype=np.float32))
    angle = positions.astype(np.float32)[..., None] / timescale.astype(np.float32)
    return np.cos(angle).astype(np.float32), np.sin(angle).astype(np.float32)


def kernel(x, ctx_1024, mask_BxS2_bk0, g_xattn, g_ffn, L0_xattn_rms_scale, L0_xattn_q_w, L0_xattn_kv_w,
           L0_xattn_out_w, L0_ffn_W1, L0_ffn_b1, L0_ffn_W2, L0_ffn_b2):
    import concourse.bacc as bacc
    from concourse.bass_utils import run_bass_kernel_spmd

    x, memory, mask = np.asarray(x), np.asarray(ctx_1024), np.asarray(mask_BxS2_bk0)
    q_w, kv_w, out_w = np.asarray(L0_xattn_q_w), np.asarray(L0_xattn_kv_w), np.asarray(L0_xattn_out_w)
    B, T, D = x.shape
    S = memory.shape[1]
    H, _, C = q_w.shape
    p, half = np.arange(P), C // 2

    q_cos, q_sin = _rotation(S + p[:, None] + P * np.arange(T // P)[None, :], half)
    k_pos = np.concatenate([np.repeat(p[:, None], B, 1), (P + p % 32)[:, None]], 1)
    k_cos, k_sin = _rotation(k_pos, half)
    power = np.float32(-(C ** -0.5))
    tables = {
        "rope_q_cos": q_cos, "rope_q_sin": np.stack([q_sin, -q_sin], 2),
        "rope_k_cos": k_cos * power, "rope_k_sin": np.stack([k_sin, -k_sin], 2) * power,
        "ident": np.eye(P, dtype=np.float32),
    }
    arrays = {
        "x": x,
        "ctx_main": memory[:, :P], "ctx_tail": memory[:, P:],
        "mask": mask,
        "gates": np.concatenate([np.asarray(g_xattn), np.asarray(g_ffn)]),
        "rms_scale": np.asarray(L0_xattn_rms_scale).reshape(D // P, P).T,
        "wq": q_w.transpose(1, 0, 2).reshape(D, H * C),
        "wk": kv_w[0, 0], "wv": kv_w[1, 0],
        "wo": out_w.transpose(1, 0, 2),
        "w1t": np.asarray(L0_ffn_W1).T, "b1": np.asarray(L0_ffn_b1).reshape(-1, P).T,
        "w2t": np.asarray(L0_ffn_W2).T, "b2": np.asarray(L0_ffn_b2),
        **tables,
    }
    arrays = {name: np.ascontiguousarray(a) for name, a in arrays.items()}
    nc = bacc.Bacc("TRN2", target_bir_lowering=False, num_devices=1)
    args = {name: nc.dram_tensor(f"in_{name}", a.shape, mybir.dt.from_np(a.dtype), kind="ExternalInput").ap()
            for name, a in arrays.items()}
    out = nc.dram_tensor("out_x", x.shape, F32, kind="ExternalOutput").ap()
    flamingo_block(nc, *args.values(), out)
    r = run_bass_kernel_spmd(nc, [{f"in_{name}": a for name, a in arrays.items()}], core_ids=[0])
    return r.results[0]["out_x"]
```

```python
from contextlib import ExitStack

import numpy as np

import concourse.bass as bass
from concourse import mybir

F32 = mybir.dt.float32
F32R = mybir.dt.float32r
U8 = mybir.dt.uint8
ALU = mybir.AluOpType
ACT = mybir.ActivationFunctionType
AX = mybir.AxisListType

P = 128
LN_EPS = 1e-5
RMS_EPS = 1e-6
MASK_FILL = -2.3819763e38
MAX_WAVELENGTH = 10000.0



def flamingo_block(nc, x, ctx_main, ctx_tail, mask, gates, rms_scale, wq, wk, wv, wo, w1t, b1, w2t, b2,
                   rope_q_cos, rope_q_sin, rope_k_cos, rope_k_sin, ident, out):
    B, T, D = x.shape
    H = wo.shape[1]
    C = wo.shape[0]
    S = mask.shape[1]
    F = w1t.shape[1]
    KD = D // P
    NT = 4
    GT = NT * P
    NG = B * T // GT
    NF = F // P
    TAIL = S - P
    TP = 32
    HP = H // 2
    CT = B + 1
    assert H * TP == P and B * TP == P and 2 * C == P and NG == 2 * B and KD == 2

    x_g = x.rearrange("b (h t p) d -> (b h) p t d", h=2, t=NT)
    out_g = out.rearrange("b (h t p) d -> (b h) p t d", h=2, t=NT)

    with ExitStack() as ctx:
        def sb(name, shape, dt=F32):
            return ctx.enter_context(nc.sbuf_tensor(name, shape, dt))

        def sem(name):
            return ctx.enter_context(nc.semaphore(name))

        ident_sb = sb("ident_sb", [P, P])
        ones_sb = sb("ones_sb", [P, P])
        neghalf = sb("neghalf", [P, 8])
        gate_raw = sb("gate_raw", [P, 2])
        gate = sb("gate", [P, 2])
        rq_cos = sb("rq_cos", [P, 2 * NT, C // 2])
        rq_sin = sb("rq_sin", [P, 2 * NT, 2, C // 2])
        rk_cos = sb("rk_cos", [P, CT, C // 2])
        rk_sin = sb("rk_sin", [P, CT, 2, C // 2])
        scale_raw = sb("scale_raw", [P, KD])
        scale1 = sb("scale1", [P, KD])
        wq_hi = sb("wq_hi", [P, KD, H * C], F32R)
        wq_lo = sb("wq_lo", [P, KD, H * C], F32R)
        wkv_raw = sb("wkv_raw", [P, KD, 3, C])
        wkv_s = sb("wkv_s", [P, KD, 3, C])
        wo_raw = sb("wo_raw", [P, H, D])
        w_tern = [sb("w1_tern", [P, KD * F], F32R), sb("w2_tern", [P, NF * D], F32R)]
        w_sums = sb("w_sums", [P, 2])
        w_scale = sb("w_scale", [P, 2])
        w_thr = sb("w_thr", [P, 2, 2])
        b1_sb = sb("b1_sb", [P, NF])
        b2_gated = sb("b2_gated", [P, D])
        mask_u8 = sb("mask_u8", [P, B, S], U8)
        mask_bias = sb("mask_bias", [P, B, S])
        mask_now = sb("mask_now", [P, S])
        ctx_bn = sb("ctx_bn", [P, CT, 6])
        ctx_mv = sb("ctx_mv", [P, CT, 2])
        ctx_ms = sb("ctx_ms", [P, CT])
        ctx_m2 = sb("ctx_m2", [P, CT])
        ctx_me = sb("ctx_me", [P, CT])
        ctx_r = sb("ctx_r", [P, CT])
        kk_hi = sb("kk_hi", [P, B, 2 * S], F32R)
        kk_lo = sb("kk_lo", [P, B, 2 * S], F32R)
        vw_hi = sb("vw_hi", [P, B, H + 1, D], F32R)
        vw_lo = sb("vw_lo", [P, B, H + 1, D], F32R)
        x_sb = [sb(f"x_sb{p}", [P, NT, D]) for p in range(2)]
        bn1 = sb("bn1", [P, NT, 6])
        mv1 = sb("mv1", [P, NT, 2])
        ve1 = sb("ve1", [P, NT])
        r1 = sb("r1", [P, NT])
        xn = sb("xn", [P, NT, D])
        xnT_hi = sb("xnT_hi", [P, KD, GT], F32R)
        xnT_lo = sb("xnT_lo", [P, KD, GT], F32R)
        q_cos = [sb(f"q_cos{j}", [P, D]) for j in range(2)]
        q_sin = [sb(f"q_sin{j}", [P, D]) for j in range(2)]
        qT_hi = [sb(f"qT_hi{j}", [P, HP, P], F32R) for j in range(2)]
        qT_lo = [sb(f"qT_lo{j}", [P, HP, P], F32R) for j in range(2)]
        s_neg = [sb(f"s_neg{j}", [P, H, S]) for j in range(2)]
        s_min = [sb(f"s_min{j}", [P, H]) for j in range(2)]
        p_sum = sb("p_sum", [P, NT, H])
        p_inv = sb("p_inv", [P, NT, H])
        pT_hi = [sb(f"pT_hi{j}", [P, H + 1, P], F32R) for j in range(2)]
        pT_lo = [sb(f"pT_lo{j}", [P, H + 1, P], F32R) for j in range(2)]
        bn2 = sb("bn2", [P, NT, 6])
        mv2 = sb("mv2", [P, NT, 2])
        ve2 = sb("ve2", [P, NT])
        r2 = sb("r2", [P, NT])
        mr2 = sb("mr2", [P, NT])
        x1nT_hi = sb("x1nT_hi", [P, KD, GT], F32R)
        x1nT_lo = sb("x1nT_lo", [P, KD, GT], F32R)

        prob = [sb(f"prob{t}", [P, H, S]) for t in range(NT)]
        prob_tail = sb("prob_tail", [P, NT, H, TP])
        x1_both = sb("x1_both", [P, 2 * NT * D])
        x1 = [x1_both[:, NT * D * p:NT * D * (p + 1)].rearrange("p (t d) -> p t d", t=NT) for p in range(2)]
        x1n = xn
        h_all = sb("h_all", [P, 4 * GT])
        h_act = [h_all[:, GT * j:GT * (j + 1)] for j in range(4)]
        hT_hi = sb("hT_hi", [P, NF, GT], F32R)
        hT_lo = sb("hT_lo", [P, NF, GT], F32R)

        class Borrow:

            def __init__(self, flat):
                self.flat, self.at = flat, 0

            def take(self, n):
                self.at += n
                return self.flat[:, self.at - n:self.at]

        w2_raw = sb("w2_raw", [P, NF * D])
        of_x1, of_w2 = Borrow(x1_both), Borrow(w2_raw)
        of_hi = Borrow(hT_hi[:].rearrange("p c t -> p (c t)"))
        of_lo = Borrow(hT_lo[:].rearrange("p c t -> p (c t)"))
        ctx_flat = of_w2.take(CT * D)
        ctx_sb = ctx_flat.rearrange("p (t d) -> p t d", t=CT)
        ctx_nT = ctx_flat.rearrange("p (k s) -> p k s", k=KD)
        k_rot = of_w2.take(CT * P).rearrange("p (t j c) -> p t j c", t=CT, j=2)
        ctx_n = of_x1.take(CT * D).rearrange("p (t d) -> p t d", t=CT)
        b2_raw = of_x1.take(D)
        k_a, k_b = (s_neg[j][:].rearrange("p h s -> p (h s)")[:, 0:CT * C].rearrange("p (t j c) -> p t j c", t=CT, j=2)
                    for j in range(2))
        wq_s = prob[0][:].rearrange("p h s -> p (h s)")[:, 0:KD * H * C].rearrange("p (k n) -> p k n", k=KD)
        wq_raw = of_x1.take(KD * H * C).rearrange("p (k n) -> p k n", k=KD)
        v_tail = of_hi.take(B * H * P).rearrange("p (b h s) -> p b h s", b=B, h=H)
        v_tmp = of_hi.take(CT * P)
        v_T = of_hi.take(CT * P)
        w_abs = of_lo.take(KD * F)
        wo_hi = of_lo.take(H * D).rearrange("p (h d) -> p h d", h=H)
        wo_lo = of_lo.take(H * D).rearrange("p (h d) -> p h d", h=H)
        w_raw = [h_all, w2_raw]
        w_low = x1_both[:, NT * D:]

        def psum(name):
            return [ctx.enter_context(nc.psum_tensor(f"{name}{j}", [P, 512], F32)) for j in range(2)]

        ps_t, ps_m, ps_s, ps_h = psum("ps_t"), psum("ps_m"), psum("ps_s"), psum("ps_h")

        ctx_in, tab_in, wkv_in, wq_in, wo_in, w_in, gate_in, mask_in, b2_in, ident_in, rope_in = (
            sem(n) for n in ("ctx_in", "tab_in", "wkv_in", "wq_in", "wo_in", "w_in", "gate_in", "mask_in",
                             "b2_in", "ident_in", "rope_in"))
        x_in = [sem("x_in0"), sem("x_in1")]
        out_done, last_out_done = [sem("out_done0"), sem("out_done1")], [sem("last_out_done0"), sem("last_out_done1")]
        const_set, ctx_zeroed, zeros_set, gate_set = (
            sem(n) for n in ("const_set", "ctx_zeroed", "zeros_set", "gate_set"))
        ctx_bn_done, ctx_stats, ctx_ms_done, ctx_rstd, ctx_normed, ctxT_filled, ctxT_copied = (
            sem(n) for n in ("ctx_bn_done", "ctx_stats", "ctx_ms_done", "ctx_rstd", "ctx_normed",
                             "ctxT_filled", "ctxT_copied"))
        scale1_set, wkv_scaled, wq_scaled, wq_hi_set, wq_set, wo_hi_set, wo_set = (
            sem(n) for n in ("scale1_set", "wkv_scaled", "wq_scaled", "wq_hi_set", "wq_set", "wo_hi_set", "wo_set"))
        k_filled, k_products, k_rotated, kT_filled, kk_hi_set, kk_set = (
            sem(n) for n in ("k_filled", "k_products", "k_rotated", "kT_filled", "kk_hi_set", "kk_set"))
        v_filled, v_hi_set, v_set, v_tail_set, vw_filled, vw_hi_set, vw_set = (
            sem(n) for n in ("v_filled", "v_hi_set", "v_set", "v_tail_set", "vw_filled", "vw_hi_set", "vw_set"))
        w_summed, w_total, w_scaled, w_thr_set, w_low_set, w_set, b2_set, mask_f_set, mask_now_set = (
            sem(n) for n in ("w_summed", "w_total", "w_scaled", "w_thr_set", "w_low_set", "w_set", "b2_set",
                             "mask_f_set", "mask_now_set"))
        t_filled, t_hi, t_lo = sem("t_filled"), sem("t_hi"), sem("t_lo")
        m_filled, m_read = sem("m_filled"), sem("m_read")
        s_filled, s_first, s_masked = sem("s_filled"), sem("s_first"), sem("s_masked")
        h_filled, h_gelu, h_split = sem("h_filled"), sem("h_gelu"), sem("h_split")
        bn1_done, ln1_stats, ln1_var, ln1_rstd, xn_done = (
            sem(n) for n in ("bn1_done", "ln1_stats", "ln1_var", "ln1_rstd", "xn_done"))
        bn2_done, ln2_stats, ln2_var, ln2_rstd, ln2_shift, x1n_done = (
            sem(n) for n in ("bn2_done", "ln2_stats", "ln2_var", "ln2_rstd", "ln2_shift", "x1n_done"))
        q_roped, exp_done, inv_done, prob_done, y_base = (
            sem(n) for n in ("q_roped", "exp_done", "inv_done", "prob_done", "y_base"))

        def has(i):
            if not isinstance(i, int):
                return True, True, True, True
            return i < NG, i + 1 < NG, 1 <= i <= NG, i >= 2

        T_ORDER = ("q0", "q1", "q2", "x1n0", "x1n1", "q3", "p0", "tail0", "p1", "tail1", "xn0", "xn1",
                   "p2", "tail2", "p3", "tail3")
        M_ORDER = ("q1", "y0", "q2", "y1", "q3", "y2", "y3", "att0", "att1", "att2", "next_q0", "att3")

        def present(order, i):
            att, nxt, f1, y = has(i)
            stage = {"q": att, "p": att, "tail": att, "att": att, "xn": nxt, "next_q": nxt, "x1n": f1, "y": y}
            return [u for u in order if stage[u[:-1]]]

        def use(order, first, i, what):
            if isinstance(i, int):
                return first + sum(len(present(order, j)) for j in range(i)) + present(order, i).index(what)
            ahead = use(order, first, 2, what) - 2 * len(order)
            return i * len(order) + ahead

        def t_use(i, what):
            return use(T_ORDER, KD, i, what)

        def m_use(i, what):
            if what == "q0":
                return 0 if isinstance(i, int) and i == 0 else use(M_ORDER, 1, i - 1, "next_q0")
            return use(M_ORDER, 1, i, what)

        def bank(banks, uses, i, what):
            return banks[uses(i if isinstance(i, int) else 2, what) % 2]

        def t_bank(i, what):
            return bank(ps_t, t_use, i, what)

        def m_bank(i, what):
            return bank(ps_m, m_use, i, what)

        def loop(eng, step, between):
            step(0, 0, 0)
            between()
            step(1, 1, 0)
            with eng.Fori(1, B - 1, 1) as b:
                step(b * 2, 0, b)
                step(b * 2 + 1, 1, b)
            for i in range(NG - 2, NG + 2):
                step(i, i % 2, i // 2)

        VW = [(b, h) for b in range(B) for h in (0, 2, None)]
        vw_banks = [ps_h[0], ps_h[1], ps_s[0], ps_s[1]]

        def vw_slot(dst, b, h):
            if h is None:
                return dst[:, b, H, :], slice(0, D)
            return dst[:, b, h:h + 2, :].rearrange("p a d -> p (a d)"), slice(0, 2 * D)

        def kk_parts(dst, rows, col):
            main = ps_s[0][rows, :].rearrange("p (b s) -> p b s", b=B)
            tails = ps_s[1][rows, 0:P].rearrange("p (b s) -> p b s", b=B)[:, :, 0:TAIL]
            return [(dst[rows, :, col:col + P], main), (dst[rows, :, col + P:col + S], tails)]

        block = ctx.enter_context(nc.Block())

        @block.sync
        def _(sp):
            sp.dma_start(ctx_sb[:, 0:B, :], ctx_main.rearrange("b p d -> p b d")).then_inc(ctx_in, 16)
            sp.wait_ge(ctx_zeroed, 1)
            for b in range(B):
                sp.dma_start(ctx_sb[TP * b:TP * b + TAIL, B, :], ctx_tail[b]).then_inc(ctx_in, 16)
            sp.dma_start(x_sb[0][:], x_g[0]).then_inc(x_in[0], 16)
            sp.dma_start(rq_cos[:], rope_q_cos).then_inc(rope_in, 16)
            sp.dma_start(rq_sin[:], rope_q_sin).then_inc(rope_in, 16)
            sp.dma_start(x_sb[1][:], x_g[1]).then_inc(x_in[1], 16)
            sp.dma_start(b1_sb[:], b1).then_inc(w_in, 16)
            sp.dma_start(w_raw[0][:].rearrange("p (k f) -> p k f", k=KD),
                         w1t.rearrange("(k p) f -> p k f", p=P)).then_inc(w_in, 16)
            sp.wait_ge(v_filled, 2)
            sp.wait_ge(kT_filled, 2)
            sp.dma_start(w_raw[1][:].rearrange("p (k f) -> p k f", k=NF),
                         w2t.rearrange("(k p) d -> p k d", p=P)).then_inc(w_in, 16)

            def step(i, p, b):
                att, _, _, y = has(i)
                if y:
                    sp.wait_ge(m_read, m_use(i, f"y{NT - 2}") + 1)
                    sp.dma_start(out_g[i - 2][:, 0:NT - 1], x1[p][:, 0:NT - 1]).then_inc(out_done[p], 16)
                    sp.wait_ge(m_read, m_use(i, f"y{NT - 1}") + 1)
                    sp.dma_start(out_g[i - 2][:, NT - 1], x1[p][:, NT - 1]).then_inc(last_out_done[p], 16)
                if att and not (isinstance(i, int) and i + 2 >= NG):
                    sp.wait_ge(bn2_done, i * NT + NT)
                    sp.dma_start(x_sb[p][:], x_g[i + 2]).then_inc(x_in[p], 16)

            loop(sp, step, lambda: None)
            for p in range(2):
                sp.wait_ge(out_done[p], 16 * B)
                sp.wait_ge(last_out_done[p], 16 * B)

        @block.gpsimd
        def _(pool):
            pool.memset(ctx_sb[:, B, :], 0.0).then_inc(ctx_zeroed, 1)
            pool.memset(neghalf[:], -0.5).then_inc(const_set, 1)
            pool.memset(ones_sb[:], 1.0).then_inc(const_set, 1)
            pool.dma_start(gate_raw[:, :], gates.partition_broadcast(P)).then_inc(gate_in, 16)
            pool.dma_start(mask_u8[:], mask.partition_broadcast(P)).then_inc(mask_in, 16)
            pool.dma_start(b2_raw, b2.partition_broadcast(P)).then_inc(b2_in, 16)

            pool.wait_ge(ctx_stats, 1)
            pool.tensor_tensor(ctx_m2[:], ctx_mv[:, :, 0], ctx_mv[:, :, 0], ALU.mult).then_inc(ctx_ms_done, 1)
            pool.wait_ge(ctx_ms_done, 1)
            pool.tensor_tensor(ctx_ms[:], ctx_m2[:], ctx_mv[:, :, 1], ALU.add).then_inc(ctx_ms_done, 1)
            pool.wait_ge(ctx_ms_done, 2)
            pool.tensor_scalar(ctx_me[:], ctx_ms[:], RMS_EPS, None, ALU.add).then_inc(ctx_ms_done, 1)
            pool.wait_ge(ctx_ms_done, 3)
            pool.wait_ge(const_set, 1)
            pool.tensor_tensor(ctx_r[:], ctx_me[:], neghalf[:, 0:CT], ALU.pow).then_inc(ctx_rstd, 1)

            def rstd(ve, r, var_sem, rstd_sem, i):
                pool.wait_ge(var_sem, i + 1)
                pool.tensor_tensor(r[:], ve[:], neghalf[:, 0:NT], ALU.pow).then_inc(rstd_sem, 1)

            rstd(ve1, r1, ln1_var, ln1_rstd, 0)
            pool.memset(prob_tail[:], 0.0).then_inc(zeros_set, 1)
            pool.memset(kk_hi[:].bitcast(F32), 0.0).then_inc(zeros_set, 1)
            pool.memset(kk_lo[:].bitcast(F32), 0.0).then_inc(zeros_set, 1)
            pool.memset(v_tail.bitcast(F32), 0.0).then_inc(zeros_set, 1)
            pool.wait_ge(wo_hi_set, 1)
            pool.tensor_tensor(wo_lo[:], wo_raw[:], wo_hi[:], ALU.subtract).then_inc(wo_set, 1)
            pool.wait_ge(v_set, 2)
            pool.wait_ge(zeros_set, 4)
            for h in range(H):
                pool.tensor_copy(v_tail[:, :, h, TP * h:TP * (h + 1)],
                                 v_T[:, B * P:].rearrange("p (b j) -> p b j", b=B)).then_inc(v_tail_set, 1)

            def rope_add(i, t):
                pool.wait_ge(m_read, m_use(i, f"q{t}") + 1)
                q = q_cos[t % 2]
                pool.tensor_tensor(q[:], q[:], q_sin[t % 2][:], ALU.add).then_inc(q_roped, 1)

            def step(i, p, b):
                att, nxt, f1, _ = has(i)

                def add_b2():
                    if f1:
                        pool.wait_ge(x1n_done, i * NT)
                        if isinstance(i, int) and i == 1:
                            pool.wait_ge(b2_set, 1)
                        b2s = b2_gated[:].rearrange("p (a d) -> p a d", a=1).to_broadcast([P, NT, D])
                        pool.tensor_tensor(x1[1 - p], x1[1 - p], b2s, ALU.add).then_inc(y_base, 1)

                if not att:
                    add_b2()
                    return

                def normalise(t):
                    pool.wait_ge(inv_done, i * NT + (t + 1))
                    inv = p_inv[:, t, :].rearrange("p (h a) -> p h a", a=1)
                    main, tail = prob[t][:, :, 0:P], prob[t][:, :, P:S]
                    pool.tensor_tensor(main, main, inv.to_broadcast([P, H, P]), ALU.mult)
                    pool.tensor_tensor(prob_tail[:, t, :, 0:TAIL], tail, inv.to_broadcast([P, H, TAIL]),
                                       ALU.mult).then_inc(prob_done, 1)

                rope_add(i, 1)
                rope_add(i, 2)
                if nxt:
                    rstd(ve1, r1, ln1_var, ln1_rstd, i + 1)
                normalise(0)
                rope_add(i, 3)
                normalise(1)
                normalise(2)
                normalise(3)
                add_b2()
                if nxt:
                    rope_add(i + 1, 0)
                rstd(ve2, r2, ln2_var, ln2_rstd, i)

            rope_add(0, 0)
            loop(pool, step, lambda: None)

        @block.scalar
        def _(act):
            act.dma_start(ident_sb[:], ident).then_inc(ident_in, 16)
            act.dma_start(scale_raw[:], rms_scale).then_inc(wkv_in, 16)
            act.dma_start(wkv_raw[:, :, 0, :], wk.rearrange("(k p) c -> p k c", p=P)).then_inc(wkv_in, 16)
            for j in (1, 2):
                act.dma_start(wkv_raw[:, :, j, :], wv.rearrange("(k p) c -> p k c", p=P)).then_inc(wkv_in, 16)
            act.dma_start(wq_raw[:], wq.rearrange("(k p) n -> p k n", p=P)).then_inc(wq_in, 16)
            act.dma_start(rk_cos[:], rope_k_cos).then_inc(tab_in, 16)
            act.dma_start(rk_sin[:], rope_k_sin).then_inc(tab_in, 16)
            for r in (0, C):
                act.dma_start(wo_raw[r:r + C], wo).then_inc(wo_in, 16)
            act.wait_ge(gate_in, 16)
            nc.scalar.activation(gate[:], gate_raw[:], ACT.Tanh).then_inc(gate_set, 1)
            act.wait_ge(wo_in, 32)
            nc.scalar.activation(wo_hi[:], wo_raw[:], ACT.Copy).then_inc(wo_hi_set, 1)
            for k in range(KD):
                act.wait_ge(ctxT_filled, k + 1)
                nc.scalar.activation(ctx_nT[:, k, 0:B * P], ps_s[k][:], ACT.Copy).then_inc(ctxT_copied, 1)
            act.wait_ge(ctxT_filled, 3)
            nc.scalar.activation(ctx_nT[:, :, B * P:], ps_h[0][:, 0:KD * P].rearrange("p (k s) -> p k s", k=KD),
                                 ACT.Copy).then_inc(ctxT_copied, 1)

            def hi_part(n, dst, src):
                act.wait_ge(t_filled, n + 1)
                nc.scalar.activation(dst, src, ACT.Copy).then_inc(t_hi, 1)

            for k in range(KD):
                hi_part(k, xnT_hi[:, k, :], ps_t[k][:])
            for n, (cols, ps) in enumerate(((slice(0, B * P), ps_m[0][:]), (slice(B * P, CT * P), ps_m[1][:, 0:P]))):
                act.wait_ge(v_filled, n + 1)
                nc.scalar.activation(v_T[0:C, cols], ps[0:C], ACT.Copy).then_inc(v_hi_set, 1)
                nc.scalar.activation(v_tmp[C:P, cols], ps[C:P], ACT.Copy).then_inc(v_hi_set, 1)
            act.wait_ge(kT_filled, 2)
            act.wait_ge(zeros_set, 3)
            for half in range(2):
                rows = slice(C * half, C * (half + 1))
                for dst, src in kk_parts(kk_hi, rows, S * half):
                    nc.scalar.activation(dst, src, ACT.Copy).then_inc(kk_hi_set, 1)
            for n, (b, h) in enumerate(VW):
                act.wait_ge(vw_filled, n + 1)
                dst, cols = vw_slot(vw_hi, b, h)
                nc.scalar.activation(dst, vw_banks[n % 4][:, cols], ACT.Copy, scale=gate[:, 0:1]).then_inc(vw_hi_set, 1)
            act.wait_ge(w_in, 16 * 3)
            for m in range(2):
                if m:
                    act.wait_ge(w_summed, m)
                nc.scalar.activation(w_abs[:], w_raw[m][:, :], ACT.Abs, accum_out=w_sums[:, m:m + 1]).then_inc(w_summed, 1)

            def step(i, p, b):
                att, nxt, f1, _ = has(i)

                def q_hi(t):
                    hi_part(t_use(i, f"q{t}"), qT_hi[t % 2][:].rearrange("p a b -> p (a b)"), t_bank(i, f"q{t}")[:, 0:D])

                def norm2():
                    if f1:
                        act.wait_ge(ln2_shift, i)
                        for t in range(NT):
                            nc.scalar.activation(x1n[:, t, :], x1[1 - p][:, t, :], ACT.Identity,
                                                 scale=r2[:, t:t + 1], bias=mr2[:, t:t + 1]).then_inc(x1n_done, 1)

                def exps(t):
                    act.wait_ge(s_masked, i * NT + (t + 1))
                    for h in range(H):
                        e = nc.scalar.activation(prob[t][:, h, :], s_neg[t % 2][:, h, :], ACT.Exp,
                                                 bias=s_min[t % 2][:, h:h + 1], scale=-1.0,
                                                 accum_out=p_sum[:, t, h:h + 1])
                    e.then_inc(exp_done, 1)

                def p_hi(t):
                    if t < 2:
                        if not (isinstance(i, int) and i == 0):
                            act.wait_ge(m_filled, m_use(i - 1, f"att{t + 2}") + 1)
                    else:
                        act.wait_ge(m_filled, m_use(i, f"att{t - 2}") + 1)
                    hi_part(t_use(i, f"p{t}"), pT_hi[t % 2][:, 0:H, :].rearrange("p h s -> p (h s)"),
                            t_bank(i, f"p{t}")[:])
                    hi_part(t_use(i, f"tail{t}"), pT_hi[t % 2][:, H, :], t_bank(i, f"tail{t}")[:, 0:P])

                def gelu(c):
                    if not f1:
                        return
                    act.wait_ge(h_filled, i * NF + (c + 1 - NF))
                    if not (isinstance(i, int) and i == 1 and c < 4):
                        act.wait_ge(h_split, i * NF + (c - 3 - NF))
                    for dst in (h_act[c % 4][:], hT_hi[:, c, :]):
                        g = nc.scalar.activation(dst, ps_h[c % 2][:], ACT.Gelu, bias=b1_sb[:, c:c + 1])
                    g.then_inc(h_gelu, 1)

                def x1n_hi():
                    if f1:
                        for k in range(KD):
                            hi_part(t_use(i, f"x1n{k}"), x1nT_hi[:, k, :], t_bank(i, f"x1n{k}")[:])

                def xn_hi():
                    if nxt:
                        for k in range(KD):
                            hi_part(t_use(i, f"xn{k}"), xnT_hi[:, k, :], t_bank(i, f"xn{k}")[:])

                if not att:
                    norm2()
                    x1n_hi()
                    for c in range(NF):
                        gelu(c)
                    return
                q_hi(0)
                norm2()
                q_hi(1)
                exps(0)
                q_hi(2)
                x1n_hi()
                exps(1)
                q_hi(3)
                exps(2)
                p_hi(0)
                exps(3)
                p_hi(1)
                xn_hi()
                gelu(0)
                gelu(1)
                p_hi(2)
                gelu(2)
                gelu(3)
                p_hi(3)
                for c in range(4, NF):
                    gelu(c)

            loop(act, step, lambda: None)

        @block.vector
        def _(dve):
            dve.wait_ge(ctx_in, 16 * (B + 1))
            for t in range(CT):
                dve.bn_stats(ctx_bn[:, t, :], ctx_sb[:, t, :]).then_inc(ctx_bn_done, 1)
            dve.wait_ge(ctx_bn_done, CT)
            for t in range(CT):
                s = dve.bn_aggr(ctx_mv[:, t, :], ctx_bn[:, t, :])
            s.then_inc(ctx_stats, 1)

            def sums1(i, p, b):
                dve.wait_ge(x_in[p], b * 16 + 16)
                for t in range(NT):
                    dve.bn_stats(bn1[:, t, :], x_sb[p][:, t, :]).then_inc(bn1_done, 1)

            def variances(i, bn, mv, stats_sem, ve, var_sem, mul, add):
                for t in range(NT):
                    s = dve.bn_aggr(mv[:, t, :], bn[:, t, :])
                s.then_inc(stats_sem, 1)
                dve.wait_ge(stats_sem, i + 1)
                dve.tensor_scalar(ve[:], mv[:, :, 1], mul, add, ALU.mult, ALU.add).then_inc(var_sem, 1)

            def variances1(i):
                variances(i, bn1, mv1, ln1_stats, ve1, ln1_var, 1.0 + RMS_EPS, LN_EPS * RMS_EPS)

            def variances2(i):
                variances(i, bn2, mv2, ln2_stats, ve2, ln2_var, 1.0, LN_EPS)

            def norm1(i, p):
                dve.wait_ge(ln1_rstd, i + 1)
                for t in range(NT):
                    dve.tensor_scalar(xn[:, t, :], x_sb[p][:, t, :], mv1[:, t, 0:1], r1[:, t:t + 1],
                                      ALU.subtract, ALU.mult).then_inc(xn_done, 1)

            def lo_part(n, dst, src, hi):
                dve.wait_ge(t_hi, n + 1)
                dve.tensor_tensor(dst, src, hi, ALU.subtract).then_inc(t_lo, 1)

            dve.wait_ge(wkv_in, 16 * 4)
            dve.tensor_scalar(scale1[:], scale_raw[:], 1.0, None, ALU.add).then_inc(scale1_set, 1)
            dve.wait_ge(scale1_set, 1)
            for k in range(KD):
                dve.tensor_scalar(wkv_s[:, k], wkv_raw[:, k], scale1[:, k:k + 1], None, ALU.mult).then_inc(wkv_scaled, 1)
            dve.wait_ge(ctx_rstd, 1)
            for t in range(CT):
                dve.tensor_scalar(ctx_n[:, t, :], ctx_sb[:, t, :], ctx_r[:, t:t + 1], None,
                                  ALU.mult).then_inc(ctx_normed, 1)
            sums1(0, 0, 0)
            dve.wait_ge(bn1_done, NT)
            variances1(0)
            dve.wait_ge(wq_in, 16)
            for k in range(KD):
                dve.tensor_scalar(wq_s[:, k], wq_raw[:, k], scale1[:, k:k + 1], None, ALU.mult).then_inc(wq_scaled, 1)
            dve.wait_ge(wq_scaled, KD)
            dve.tensor_copy(wq_hi[:], wq_s).then_inc(wq_hi_set, 1)
            dve.wait_ge(wq_hi_set, 1)
            dve.tensor_tensor(wq_lo[:], wq_s, wq_hi[:], ALU.subtract).then_inc(wq_set, 1)
            norm1(0, 0)
            dve.wait_ge(k_filled, 1)
            dve.wait_ge(tab_in, 32)
            kps = ps_h[1][:, 0:CT * C].rearrange("p (t j c) -> p t j c", t=CT, j=2)
            for j in range(2):
                dve.tensor_tensor(k_a[:, :, j, :], kps[:, :, j, :], rk_cos[:], ALU.mult).then_inc(k_products, 1)
                dve.tensor_tensor(k_b[:, :, 1 - j, :], kps[:, :, j, :], rk_sin[:, :, j, :],
                                  ALU.mult).then_inc(k_products, 1)
            dve.wait_ge(k_products, 4)
            for j in range(2):
                dve.tensor_tensor(k_rot[:, :, j, :], k_a[:].rearrange("p t j c -> p t (j c)"),
                                  k_b[:].rearrange("p t j c -> p t (j c)"), ALU.add).then_inc(k_rotated, 1)
            for k in range(KD):
                lo_part(k, xnT_lo[:, k, :], ps_t[k][:], xnT_hi[:, k, :])
            for n, (cols, ps) in enumerate(((slice(0, B * P), ps_m[0][:]), (slice(B * P, CT * P), ps_m[1][:, 0:P]))):
                dve.wait_ge(v_hi_set, 2 * n + 2)
                dve.tensor_tensor(v_T[C:P, cols], ps[C:P], v_tmp[C:P, cols], ALU.subtract).then_inc(v_set, 1)
            dve.wait_ge(kk_hi_set, 4)
            for half in range(2):
                rows = slice(C * half, C * (half + 1))
                for (dst, src), (hi, _) in zip(kk_parts(kk_lo, rows, S * half), kk_parts(kk_hi, rows, S * half)):
                    dve.tensor_tensor(dst, src, hi, ALU.subtract).then_inc(kk_set, 1)
            dve.wait_ge(mask_in, 16)
            dve.tensor_scalar(mask_bias[:], mask_u8[:], MASK_FILL, -MASK_FILL, ALU.mult, ALU.add).then_inc(mask_f_set, 1)
            dve.wait_ge(gate_set, 1)
            dve.wait_ge(b2_in, 16)
            dve.tensor_scalar(b2_gated[:], b2_raw, gate[:, 1:2], None, ALU.mult).then_inc(b2_set, 1)
            for n, (b, h) in enumerate(VW):
                dve.wait_ge(vw_hi_set, n + 1)
                hi, cols = vw_slot(vw_hi, b, h)
                dve.scalar_tensor_tensor(vw_slot(vw_lo, b, h)[0], vw_banks[n % 4][:, cols], gate[:, 0:1], hi,
                                         ALU.mult, ALU.subtract).then_inc(vw_set, 1)
            dve.wait_ge(mask_f_set, 1)
            dve.wait_ge(rope_in, 32)

            def ternary():
                dve.wait_ge(w_total, 1)
                dve.tensor_scalar(w_scale[:], ps_h[0][:, 0:2], 1.0 / (D * F), 1e-8, ALU.mult,
                                  ALU.max).then_inc(w_scaled, 1)
                dve.wait_ge(w_scaled, 1)
                for n, sign in enumerate((0.5, -0.5)):
                    dve.tensor_scalar(w_thr[:, n, :], w_scale[:], sign, None, ALU.mult).then_inc(w_thr_set, 1)
                dve.wait_ge(w_thr_set, 2)
                for n in range(4):
                    m, cols = n // 2, slice(n % 2 * NT * D, (n % 2 + 1) * NT * D)
                    if n:
                        dve.wait_ge(w_set, n)
                    dve.tensor_scalar(w_low, w_raw[m][:, cols], w_thr[:, 1, m:m + 1], None,
                                      ALU.is_lt).then_inc(w_low_set, 1)
                    dve.wait_ge(w_low_set, n + 1)
                    dve.scalar_tensor_tensor(w_tern[m][:, cols], w_raw[m][:, cols], w_thr[:, 0, m:m + 1], w_low,
                                             ALU.is_gt, ALU.subtract).then_inc(w_set, 1)

            def rope(i, p, t):
                n = m_use(i, f"q{t}")
                dve.wait_ge(m_filled, n + 1)
                q = m_bank(i, f"q{t}")[:, 0:D]
                pos = NT * p + t
                cos = rq_cos[:, pos, :].rearrange("p (a c) -> p a c", a=1).to_broadcast([P, 2 * H, C // 2])
                dve.tensor_tensor(q_cos[t % 2][:].rearrange("p (a c) -> p a c", a=2 * H),
                                  q.rearrange("p (a c) -> p a c", a=2 * H), cos, ALU.mult)
                sin = rq_sin[:, pos].rearrange("p (a j) c -> p a j c", a=1).to_broadcast([P, H, 2, C // 2])
                dve.tensor_tensor(q_sin[t % 2][:].rearrange("p (h j c) -> p h j c", h=H, j=2)[:, :, ::-1, :],
                                  q.rearrange("p (h j c) -> p h j c", h=H, j=2), sin,
                                  ALU.mult).then_inc(m_read, 1)

            def step(i, p, b):
                att, nxt, f1, y = has(i)

                def q_lo(t):
                    lo_part(t_use(i, f"q{t}"), qT_lo[t % 2][:].rearrange("p a b -> p (a b)"),
                            t_bank(i, f"q{t}")[:, 0:D], qT_hi[t % 2][:].rearrange("p a b -> p (a b)"))

                def mask_and_min(t):
                    dve.wait_ge(s_filled, i * NT + (t + 1))
                    s, least = s_neg[t % 2], s_min[t % 2]
                    dve.tensor_tensor(s[:, 0, :], ps_s[0][:, 0:S], mask_now[:], ALU.add).then_inc(s_first, 1)
                    for h in range(1, H):
                        dve.tensor_tensor_reduce(
                            s[:, h, :], ps_s[h // 2][:, S * (h % 2):S * (h % 2 + 1)], mask_now[:],
                            1.0, 3.4e38, ALU.add, ALU.min, least[:, h:h + 1])
                    dve.wait_ge(s_first, i * NT + (t + 1))
                    dve.tensor_reduce(least[:, 0:1], s[:, 0, :], AX.X, ALU.min).then_inc(s_masked, 1)

                def inverse(t):
                    dve.wait_ge(exp_done, i * NT + (t + 1))
                    dve.reciprocal(p_inv[:, t, :], p_sum[:, t, :]).then_inc(inv_done, 1)

                def ffn_out(t):
                    if not y:
                        return
                    n = m_use(i, f"y{t}")
                    dve.wait_ge(m_filled, n + 1)
                    dve.wait_ge(y_base, i - 1)
                    ys = x1[p][:, t, :]
                    dve.scalar_tensor_tensor(ys, m_bank(i, f"y{t}")[:, 0:D], gate[:, 1:2], ys,
                                             ALU.mult, ALU.add).then_inc(m_read, 1)

                def p_lo(t):
                    lo_part(t_use(i, f"p{t}"), pT_lo[t % 2][:, 0:H, :].rearrange("p h s -> p (h s)"),
                            t_bank(i, f"p{t}")[:], pT_hi[t % 2][:, 0:H, :].rearrange("p h s -> p (h s)"))
                    lo_part(t_use(i, f"tail{t}"), pT_lo[t % 2][:, H, :], t_bank(i, f"tail{t}")[:, 0:P],
                            pT_hi[t % 2][:, H, :])

                def residual(t):
                    n = m_use(i, f"att{t}")
                    dve.wait_ge(m_filled, n + 1)
                    if t in (0, NT - 1) and not (isinstance(i, int) and i < 2):
                        dve.wait_ge((out_done if t == 0 else last_out_done)[p], b * 16)
                    dve.tensor_tensor(x1[p][:, t, :], m_bank(i, f"att{t}")[:, 0:D], x_sb[p][:, t, :],
                                      ALU.add).then_inc(m_read, 1)
                    dve.wait_ge(m_read, n + 1)
                    dve.bn_stats(bn2[:, t, :], x1[p][:, t, :]).then_inc(bn2_done, 1)

                def split_h(c):
                    if not f1:
                        return
                    g = i * NF + (c + 1 - NF)
                    dve.wait_ge(h_gelu, g)
                    dve.tensor_tensor(hT_lo[:, c, :], h_act[c % 4][:], hT_hi[:, c, :], ALU.subtract).then_inc(h_split, 1)

                def x1n_lo():
                    if f1:
                        for k in range(KD):
                            lo_part(t_use(i, f"x1n{k}"), x1nT_lo[:, k, :], t_bank(i, f"x1n{k}")[:], x1nT_hi[:, k, :])

                def xn_lo():
                    if nxt:
                        for k in range(KD):
                            lo_part(t_use(i, f"xn{k}"), xnT_lo[:, k, :], t_bank(i, f"xn{k}")[:], xnT_hi[:, k, :])

                def shift2():
                    if f1:
                        """-mean * rstd of group i - 1."""
                        dve.wait_ge(ln2_rstd, i)
                        dve.scalar_tensor_tensor(mr2[:], mv2[:, :, 0], -1.0, r2[:], ALU.mult,
                                                 ALU.mult).then_inc(ln2_shift, 1)

                if not att:
                    shift2()
                    for t in range(NT - 1):
                        ffn_out(t)
                    x1n_lo()
                    ffn_out(NT - 1)
                    for c in range(NF):
                        split_h(c)
                    return

                q_lo(0)
                rope(i, p, 1)
                if p == 0:
                    dve.tensor_copy(mask_now[:], mask_bias[:, b, :]).then_inc(mask_now_set, 1)
                shift2()
                if nxt:
                    sums1(i + 1, 1 - p, b if p == 0 else b + 1)
                ffn_out(0)
                if nxt:
                    dve.wait_ge(bn1_done, i * NT + 2 * NT)
                q_lo(1)
                if p == 0:
                    dve.wait_ge(mask_now_set, b + 1)
                mask_and_min(0)
                rope(i, p, 2)
                if nxt:
                    variances1(i + 1)
                ffn_out(1)
                q_lo(2)
                mask_and_min(1)
                inverse(0)
                rope(i, p, 3)
                x1n_lo()
                ffn_out(2)
                mask_and_min(2)
                q_lo(3)
                inverse(1)
                ffn_out(3)
                mask_and_min(3)
                p_lo(0)
                inverse(2)
                if nxt:
                    norm1(i + 1, 1 - p)
                p_lo(1)
                inverse(3)
                residual(0)
                xn_lo()
                residual(1)
                split_h(0)
                split_h(1)
                p_lo(2)
                split_h(2)
                split_h(3)
                residual(2)
                p_lo(3)
                for c in range(4, NF - 1):
                    split_h(c)
                if nxt:
                    rope(i + 1, 1 - p, 0)
                residual(3)
                dve.wait_ge(bn2_done, i * NT + NT)
                split_h(7)
                variances2(i)

            rope(0, 0, 0)
            loop(dve, step, ternary)

        @block.tensor
        def _(pe):
            def products(dst, pairs):
                for n, (lhs, rhs) in enumerate(pairs):
                    m = pe.matmul(dst, lhs, rhs, start=(n == 0), stop=(n == len(pairs) - 1))
                return m

            def transposed_tiles(n, dst, src, k):
                if not (isinstance(n, int) and n < 2):
                    pe.wait_ge(t_lo, n - 1)
                for t in range(NT):
                    m = pe.transpose(dst[:, P * t:P * (t + 1)], src[:, t, P * k:P * (k + 1)], ident_sb[:])
                m.then_inc(t_filled, 1)

            pe.wait_ge(ident_in, 16)
            pe.wait_ge(ctx_normed, CT)
            for k in range(KD):
                for t in range(B):
                    m = pe.transpose(ps_s[k][:, P * t:P * (t + 1)], ctx_n[:, t, P * k:P * (k + 1)], ident_sb[:])
                m.then_inc(ctxT_filled, 1)
            for k in range(KD):
                m = pe.transpose(ps_h[0][:, P * k:P * (k + 1)], ctx_n[:, B, P * k:P * (k + 1)], ident_sb[:])
            m.then_inc(ctxT_filled, 1)
            pe.wait_ge(xn_done, NT)
            for k in range(KD):
                transposed_tiles(k, ps_t[k], xn, k)
            pe.wait_ge(wkv_scaled, KD)
            pe.wait_ge(ctxT_copied, 3)
            for t in range(CT):
                m = products(ps_h[1][:, C * t:C * (t + 1)],
                             [(ctx_nT[:, k, P * t:P * (t + 1)], wkv_s[:, k, 0, :]) for k in range(KD)])
            m.then_inc(k_filled, 1)
            for cols, dst in ((slice(0, B * P), ps_m[0][:]), (slice(B * P, CT * P), ps_m[1][:, 0:P])):
                products(dst, [(wkv_s[:, k, 1:3, :].rearrange("p a c -> p (a c)"), ctx_nT[:, k, cols])
                               for k in range(KD)]).then_inc(v_filled, 1)
            pe.wait_ge(k_rotated, 2)
            for t in range(CT):
                dst = ps_s[0][:, P * t:P * (t + 1)] if t < B else ps_s[1][:, 0:P]
                m = pe.transpose(dst, k_rot[:, t].rearrange("p j c -> p (j c)"), ident_sb[:])
                if t >= B - 1:
                    m.then_inc(kT_filled, 1)
            pe.wait_ge(v_set, 2)
            pe.wait_ge(wo_set, 1)
            for n, (b, h) in enumerate(VW):
                if n == 2:
                    pe.wait_ge(v_tail_set, H)
                    pe.wait_ge(kk_set, 4)
                if n >= 4:
                    pe.wait_ge(vw_set, n - 3)
                if h is None:
                    pairs = [(v_tail[:, b, j, :], w[:, j, :]) for w in (wo_hi, wo_lo) for j in range(H)]
                else:
                    pairs = [(v_T[:, P * b:P * (b + 1)], w[:, h:h + 2, :].rearrange("p a d -> p (a d)"))
                             for w in (wo_hi, wo_lo)]
                products(vw_banks[n % 4][:, vw_slot(vw_hi, b, h)[1]], pairs).then_inc(vw_filled, 1)
            pe.wait_ge(wq_set, 1)
            pe.wait_ge(vw_set, len(VW))

            def sum_weights():
                pe.wait_ge(w_summed, 2)
                pe.wait_ge(const_set, 2)
                pe.matmul(ps_h[0][:, 0:2], ones_sb[:], w_sums[:], start=True, stop=True).then_inc(w_total, 1)

            def bank_m(i, what):
                n = m_use(i, what)
                if not (isinstance(n, int) and n < 2):
                    pe.wait_ge(m_read, n - 1)
                return m_bank(i, what)[:, 0:D]

            def q(i, t):
                tile = slice(P * t, P * (t + 1))
                products(bank_m(i, f"q{t}"), [(a[:, k, tile], w[:, k, :]) for k in range(KD)
                                              for a, w in ((xnT_hi, wq_hi), (xnT_hi, wq_lo), (xnT_lo, wq_hi))]
                         ).then_inc(m_filled, 1)

            def step(i, p, b):
                att, nxt, f1, y = has(i)

                def q_T(t):
                    if not att:
                        return
                    n = t_use(i, f"q{t}")
                    pe.wait_ge(t_lo, n - 1)
                    pe.wait_ge(q_roped, i * NT + (t + 1))
                    for a in range(HP):
                        m = pe.transpose(t_bank(i, f"q{t}")[:, P * a:P * (a + 1)], q_cos[t % 2][:, P * a:P * (a + 1)],
                                         ident_sb[:])
                    m.then_inc(t_filled, 1)

                def scores(t):
                    if not att:
                        return
                    pe.wait_ge(t_lo, t_use(i, f"q{t}") + 1)
                    if not (isinstance(i, int) and i == 0 and t == 0):
                        pe.wait_ge(s_masked, i * NT + t)
                    for a in range(HP):
                        m = products(ps_s[a][:, 0:2 * S],
                                     [(qT_hi[t % 2][:, a, :], kk_hi[:, b, :]), (qT_hi[t % 2][:, a, :], kk_lo[:, b, :]),
                                      (qT_lo[t % 2][:, a, :], kk_hi[:, b, :])])
                    m.then_inc(s_filled, 1)

                def p_T(t):
                    if not att:
                        return
                    pe.wait_ge(prob_done, i * NT + (t + 1))
                    n = t_use(i, f"p{t}")
                    pe.wait_ge(t_lo, n - 1)
                    for h in range(H):
                        m = pe.transpose(t_bank(i, f"p{t}")[:, P * h:P * (h + 1)], prob[t][:, h, 0:P], ident_sb[:])
                    m.then_inc(t_filled, 1)
                    pe.wait_ge(t_lo, n)
                    pe.transpose(t_bank(i, f"tail{t}")[:, 0:P], prob_tail[:, t].rearrange("p h s -> p (h s)"), ident_sb[:]).then_inc(t_filled, 1)

                def attend(t):
                    if not att:
                        return
                    pe.wait_ge(t_lo, t_use(i, f"tail{t}") + 1)
                    dst = bank_m(i, f"att{t}")
                    hi, lo = pT_hi[t % 2], pT_lo[t % 2]
                    products(dst, [(a[:, c, :], w[:, b, c, :]) for c in range(H + 1)
                                   for a, w in ((hi, vw_hi), (hi, vw_lo), (lo, vw_hi))]).then_inc(m_filled, 1)

                def x1_T():
                    if f1:
                        pe.wait_ge(x1n_done, i * NT)
                        for k in range(KD):
                            transposed_tiles(t_use(i, f"x1n{k}"), t_bank(i, f"x1n{k}"), x1n, k)

                def ffn_in(c):
                    if not f1:
                        return
                    if c == 0:
                        pe.wait_ge(t_lo, t_use(i, "x1n1") + 1)
                        if isinstance(i, int) and i == 1:
                            pe.wait_ge(w_set, 4)
                    if not (isinstance(i, int) and i == 1 and c < 2):
                        pe.wait_ge(h_gelu, i * NF + (c - 1 - NF))
                    w = w_tern[0][:].rearrange("p (k f) -> p k f", k=KD)
                    products(ps_h[c % 2][:], [(w[:, k, P * c:P * (c + 1)], a[:, k, :]) for k in range(KD)
                                              for a in (x1nT_hi, x1nT_lo)]).then_inc(h_filled, 1)

                def ffn_out(t):
                    if not y:
                        return
                    w = w_tern[1][:].rearrange("p (c d) -> p c d", c=NF)
                    dst = bank_m(i, f"y{t}")
                    for c in range(NF):
                        if t == 0 and c in (0, NF - 2):
                            pe.wait_ge(h_split, (i - 1) * NF - (2 if c == 0 else 0))
                        for a in (hT_hi, hT_lo):
                            m = pe.matmul(dst, a[:, c, P * t:P * (t + 1)], w[:, c, :],
                                          start=(c == 0 and a is hT_hi), stop=(c == NF - 1 and a is hT_lo))
                    m.then_inc(m_filled, 1)

                def xn_T():
                    if nxt:
                        pe.wait_ge(xn_done, i * NT + 2 * NT)
                        for k in range(KD):
                            transposed_tiles(t_use(i, f"xn{k}"), t_bank(i, f"xn{k}"), xn, k)

                if not att:
                    for t in range(NT - 1):
                        ffn_out(t)
                    x1_T()
                    ffn_out(NT - 1)
                    for c in range(NF):
                        ffn_in(c)
                    return
                q_T(0)
                q(i, 1)
                ffn_out(0)
                scores(0)
                q_T(1)
                q(i, 2)
                ffn_out(1)
                scores(1)
                q_T(2)
                q(i, 3)
                x1_T()
                ffn_out(2)
                scores(2)
                q_T(3)
                ffn_out(3)
                scores(3)
                p_T(0)
                ffn_in(0)
                ffn_in(1)
                p_T(1)
                attend(0)
                xn_T()
                attend(1)
                p_T(2)
                ffn_in(2)
                ffn_in(3)
                attend(2)
                p_T(3)
                for c in range(4, NF):
                    ffn_in(c)
                if nxt:
                    pe.wait_ge(t_lo, t_use(i, "xn1") + 1)
                    q(i + 1, 0)
                attend(3)

            pe.wait_ge(t_lo, KD)
            q(0, 0)
            loop(pe, step, sum_weights)


def _rotation(positions, half):
    timescale = np.float32(MAX_WAVELENGTH) ** (np.float32(1.0 / half) * np.arange(half, dtype=np.float32))
    angle = positions.astype(np.float32)[..., None] / timescale.astype(np.float32)
    return np.cos(angle).astype(np.float32), np.sin(angle).astype(np.float32)


def kernel(x, ctx_1024, mask_BxS2_bk0, g_xattn, g_ffn, L0_xattn_rms_scale, L0_xattn_q_w, L0_xattn_kv_w,
           L0_xattn_out_w, L0_ffn_W1, L0_ffn_b1, L0_ffn_W2, L0_ffn_b2):
    import concourse.bacc as bacc
    from concourse.bass_utils import run_bass_kernel_spmd

    x, memory, mask = np.asarray(x), np.asarray(ctx_1024), np.asarray(mask_BxS2_bk0)
    q_w, kv_w, out_w = np.asarray(L0_xattn_q_w), np.asarray(L0_xattn_kv_w), np.asarray(L0_xattn_out_w)
    B, T, D = x.shape
    S = memory.shape[1]
    H, _, C = q_w.shape
    p, half = np.arange(P), C // 2

    q_cos, q_sin = _rotation(S + p[:, None] + P * np.arange(T // P)[None, :], half)
    k_pos = np.concatenate([np.repeat(p[:, None], B, 1), (P + p % 32)[:, None]], 1)
    k_cos, k_sin = _rotation(k_pos, half)
    power = np.float32(-(C ** -0.5))
    tables = {
        "rope_q_cos": q_cos, "rope_q_sin": np.stack([q_sin, -q_sin], 2),
        "rope_k_cos": k_cos * power, "rope_k_sin": np.stack([k_sin, -k_sin], 2) * power,
        "ident": np.eye(P, dtype=np.float32),
    }
    arrays = {
        "x": x,
        "ctx_main": memory[:, :P], "ctx_tail": memory[:, P:],
        "mask": mask,
        "gates": np.concatenate([np.asarray(g_xattn), np.asarray(g_ffn)]),
        "rms_scale": np.asarray(L0_xattn_rms_scale).reshape(D // P, P).T,
        "wq": q_w.transpose(1, 0, 2).reshape(D, H * C),
        "wk": kv_w[0, 0], "wv": kv_w[1, 0],
        "wo": out_w.transpose(1, 0, 2),
        "w1t": np.asarray(L0_ffn_W1).T, "b1": np.asarray(L0_ffn_b1).reshape(-1, P).T,
        "w2t": np.asarray(L0_ffn_W2).T, "b2": np.asarray(L0_ffn_b2),
        **tables,
    }
    arrays = {name: np.ascontiguousarray(a) for name, a in arrays.items()}
    nc = bacc.Bacc("TRN2", target_bir_lowering=False, num_devices=1)
    args = {name: nc.dram_tensor(f"in_{name}", a.shape, mybir.dt.from_np(a.dtype), kind="ExternalInput").ap()
            for name, a in arrays.items()}
    out = nc.dram_tensor("out_x", x.shape, F32, kind="ExternalOutput").ap()
    flamingo_block(nc, *args.values(), out)
    r = run_bass_kernel_spmd(nc, [{f"in_{name}": a for name, a in arrays.items()}], core_ids=[0])
    return r.results[0]["out_x"]
```

```python
from contextlib import ExitStack

import numpy as np

import concourse.bass as bass
from concourse import mybir

F32 = mybir.dt.float32
F32R = mybir.dt.float32r
U8 = mybir.dt.uint8
ALU = mybir.AluOpType
ACT = mybir.ActivationFunctionType
AX = mybir.AxisListType

P = 128
LN_EPS = 1e-5
RMS_EPS = 1e-6
MASK_FILL = -2.3819763e38
MAX_WAVELENGTH = 10000.0



def flamingo_block(nc, x, ctx_main, ctx_tail, mask, gates, rms_scale, wq, wk, wv, wo, w1t, b1, w2t, b2,
                   rope_q_cos, rope_q_sin, rope_k_cos, rope_k_sin, ident, out):
    B, T, D = x.shape
    H = wo.shape[1]
    C = wo.shape[0]
    S = mask.shape[1]
    F = w1t.shape[1]
    KD = D // P
    NT = 4
    GT = NT * P
    NG = B * T // GT
    NF = F // P
    TAIL = S - P
    TP = 32
    HP = H // 2
    CT = B + 1
    assert H * TP == P and B * TP == P and 2 * C == P and NG == 2 * B and KD == 2

    x_g = x.rearrange("b (h t p) d -> (b h) p t d", h=2, t=NT)
    out_g = out.rearrange("b (h t p) d -> (b h) p t d", h=2, t=NT)

    with ExitStack() as ctx:
        def sb(name, shape, dt=F32):
            return ctx.enter_context(nc.sbuf_tensor(name, shape, dt))

        def sem(name):
            return ctx.enter_context(nc.semaphore(name))

        ident_sb = sb("ident_sb", [P, P])
        ones_sb = sb("ones_sb", [P, P])
        neghalf = sb("neghalf", [P, 8])
        exp_warm = sb("exp_warm", [P, 1])
        gate_raw = sb("gate_raw", [P, 2])
        gate = sb("gate", [P, 2])
        rq_cos = sb("rq_cos", [P, 2 * NT, C // 2])
        rq_sin = sb("rq_sin", [P, 2 * NT, 2, C // 2])
        rk_cos = sb("rk_cos", [P, CT, C // 2])
        rk_sin = sb("rk_sin", [P, CT, 2, C // 2])
        scale_raw = sb("scale_raw", [P, KD])
        scale1 = sb("scale1", [P, KD])
        wq_hi = sb("wq_hi", [P, KD, H * C], F32R)
        wq_lo = sb("wq_lo", [P, KD, H * C], F32R)
        wkv_raw = sb("wkv_raw", [P, KD, 3, C])
        wkv_s = sb("wkv_s", [P, KD, 3, C])
        wo_raw = sb("wo_raw", [P, H, D])
        w_tern = [sb("w1_tern", [P, KD * F], F32R), sb("w2_tern", [P, NF * D], F32R)]
        w_sums = sb("w_sums", [P, 2])
        w_scale = sb("w_scale", [P, 2])
        w_thr = sb("w_thr", [P, 2, 2])
        b1_sb = sb("b1_sb", [P, NF])
        b2_gated = sb("b2_gated", [P, D])
        mask_u8 = sb("mask_u8", [P, B, S], U8)
        mask_bias = sb("mask_bias", [P, B, S])
        mask_now = sb("mask_now", [P, S])
        ctx_bn = sb("ctx_bn", [P, CT, 6])
        ctx_mv = sb("ctx_mv", [P, CT, 2])
        ctx_ms = sb("ctx_ms", [P, CT])
        ctx_m2 = sb("ctx_m2", [P, CT])
        ctx_me = sb("ctx_me", [P, CT])
        ctx_r = sb("ctx_r", [P, CT])
        kk_hi = sb("kk_hi", [P, B, 2 * S], F32R)
        kk_lo = sb("kk_lo", [P, B, 2 * S], F32R)
        vw_hi = sb("vw_hi", [P, B, H + 1, D], F32R)
        vw_lo = sb("vw_lo", [P, B, H + 1, D], F32R)
        x_sb = [sb(f"x_sb{p}", [P, NT, D]) for p in range(2)]
        bn1 = sb("bn1", [P, NT, 6])
        mv1 = sb("mv1", [P, NT, 2])
        ve1 = sb("ve1", [P, NT])
        r1 = sb("r1", [P, NT])
        xn = sb("xn", [P, NT, D])
        xnT_hi = sb("xnT_hi", [P, KD, GT], F32R)
        xnT_lo = sb("xnT_lo", [P, KD, GT], F32R)
        q_cos = [sb(f"q_cos{j}", [P, D]) for j in range(2)]
        q_sin = [sb(f"q_sin{j}", [P, D]) for j in range(2)]
        qT_hi = [sb(f"qT_hi{j}", [P, HP, P], F32R) for j in range(2)]
        qT_lo = [sb(f"qT_lo{j}", [P, HP, P], F32R) for j in range(2)]
        s_neg = [sb(f"s_neg{j}", [P, H, S]) for j in range(2)]
        s_min = [sb(f"s_min{j}", [P, H]) for j in range(2)]
        p_sum = sb("p_sum", [P, NT, H])
        p_inv = sb("p_inv", [P, NT, H])
        pT_hi = [sb(f"pT_hi{j}", [P, H + 1, P], F32R) for j in range(2)]
        pT_lo = [sb(f"pT_lo{j}", [P, H + 1, P], F32R) for j in range(2)]
        bn2 = sb("bn2", [P, NT, 6])
        mv2 = sb("mv2", [P, NT, 2])
        ve2 = sb("ve2", [P, NT])
        r2 = sb("r2", [P, NT])
        mr2 = sb("mr2", [P, NT])
        x1nT_hi = sb("x1nT_hi", [P, KD, GT], F32R)
        x1nT_lo = sb("x1nT_lo", [P, KD, GT], F32R)

        prob = [sb(f"prob{t}", [P, H, S]) for t in range(NT)]
        prob_tail = sb("prob_tail", [P, NT, H, TP])
        x1_both = sb("x1_both", [P, 2 * NT * D])
        x1 = [x1_both[:, NT * D * p:NT * D * (p + 1)].rearrange("p (t d) -> p t d", t=NT) for p in range(2)]
        x1n = xn
        h_all = sb("h_all", [P, 4 * GT])
        h_act = [h_all[:, GT * j:GT * (j + 1)] for j in range(4)]
        hT_hi = sb("hT_hi", [P, NF, GT], F32R)
        hT_lo = sb("hT_lo", [P, NF, GT], F32R)

        class Borrow:

            def __init__(self, flat):
                self.flat, self.at = flat, 0

            def take(self, n):
                self.at += n
                return self.flat[:, self.at - n:self.at]

        w2_raw = sb("w2_raw", [P, NF * D])
        of_x1, of_w2 = Borrow(x1_both), Borrow(w2_raw)
        of_hi = Borrow(hT_hi[:].rearrange("p c t -> p (c t)"))
        of_lo = Borrow(hT_lo[:].rearrange("p c t -> p (c t)"))
        ctx_flat = of_w2.take(CT * D)
        ctx_sb = ctx_flat.rearrange("p (t d) -> p t d", t=CT)
        ctx_nT = ctx_flat.rearrange("p (k s) -> p k s", k=KD)
        k_rot = of_w2.take(CT * P).rearrange("p (t j c) -> p t j c", t=CT, j=2)
        ctx_n = of_x1.take(CT * D).rearrange("p (t d) -> p t d", t=CT)
        b2_raw = of_x1.take(D)
        k_a, k_b = (s_neg[j][:].rearrange("p h s -> p (h s)")[:, 0:CT * C].rearrange("p (t j c) -> p t j c", t=CT, j=2)
                    for j in range(2))
        wq_s = prob[0][:].rearrange("p h s -> p (h s)")[:, 0:KD * H * C].rearrange("p (k n) -> p k n", k=KD)
        wq_raw = of_x1.take(KD * H * C).rearrange("p (k n) -> p k n", k=KD)
        v_tail = of_hi.take(B * H * P).rearrange("p (b h s) -> p b h s", b=B, h=H)
        v_tmp = of_hi.take(CT * P)
        v_T = of_hi.take(CT * P)
        w_abs = of_lo.take(KD * F)
        wo_hi = of_lo.take(H * D).rearrange("p (h d) -> p h d", h=H)
        wo_lo = of_lo.take(H * D).rearrange("p (h d) -> p h d", h=H)
        w_raw = [h_all, w2_raw]
        w_low = [w_abs[:, GT * j:GT * (j + 1)] for j in range(NT)] + [
            x1_both[:, NT * D + GT * j:NT * D + GT * (j + 1)] for j in range(2)]
        NL = len(w_low)

        def psum(name):
            return [ctx.enter_context(nc.psum_tensor(f"{name}{j}", [P, 512], F32)) for j in range(2)]

        ps_t, ps_m, ps_s, ps_h = psum("ps_t"), psum("ps_m"), psum("ps_s"), psum("ps_h")

        ctx_in, tab_in, wkv_in, wq_in, wo_in, w_in, gate_in, mask_in, b2_in, ident_in, rope_in = (
            sem(n) for n in ("ctx_in", "tab_in", "wkv_in", "wq_in", "wo_in", "w_in", "gate_in", "mask_in",
                             "b2_in", "ident_in", "rope_in"))
        x_in = [sem("x_in0"), sem("x_in1")]
        out_done, last_out_done = [sem("out_done0"), sem("out_done1")], [sem("last_out_done0"), sem("last_out_done1")]
        const_set, ctx_zeroed, zeros_set, gate_set = (
            sem(n) for n in ("const_set", "ctx_zeroed", "zeros_set", "gate_set"))
        ctx_bn_done, ctx_stats, ctx_ms_done, ctx_rstd, ctx_normed, ctxT_filled, ctxT_copied = (
            sem(n) for n in ("ctx_bn_done", "ctx_stats", "ctx_ms_done", "ctx_rstd", "ctx_normed",
                             "ctxT_filled", "ctxT_copied"))
        scale1_set, wkv_scaled, wq_scaled, wq_hi_set, wq_set, wo_hi_set, wo_set = (
            sem(n) for n in ("scale1_set", "wkv_scaled", "wq_scaled", "wq_hi_set", "wq_set", "wo_hi_set", "wo_set"))
        k_filled, k_products, k_rotated, kT_filled, kk_hi_set, kk_set = (
            sem(n) for n in ("k_filled", "k_products", "k_rotated", "kT_filled", "kk_hi_set", "kk_set"))
        v_filled, v_hi_set, v_set, v_tail_set, vw_filled, vw_hi_set, vw_set = (
            sem(n) for n in ("v_filled", "v_hi_set", "v_set", "v_tail_set", "vw_filled", "vw_hi_set", "vw_set"))
        w_summed, w_total, w_scaled, w_thr_set, w_low_set, w_set, b2_set, mask_f_set, mask_now_set = (
            sem(n) for n in ("w_summed", "w_total", "w_scaled", "w_thr_set", "w_low_set", "w_set", "b2_set",
                             "mask_f_set", "mask_now_set"))
        t_filled, t_hi, t_lo = sem("t_filled"), sem("t_hi"), sem("t_lo")
        m_filled, m_read = sem("m_filled"), sem("m_read")
        s_filled, s_first, s_masked = sem("s_filled"), sem("s_first"), sem("s_masked")
        h_filled, h_gelu, h_split = sem("h_filled"), sem("h_gelu"), sem("h_split")
        bn1_done, ln1_stats, ln1_var, ln1_rstd, xn_done = (
            sem(n) for n in ("bn1_done", "ln1_stats", "ln1_var", "ln1_rstd", "xn_done"))
        bn2_done, ln2_stats, ln2_var, ln2_rstd, ln2_shift, x1n_done = (
            sem(n) for n in ("bn2_done", "ln2_stats", "ln2_var", "ln2_rstd", "ln2_shift", "x1n_done"))
        q_roped, exp_done, inv_done, prob_done, y_base = (
            sem(n) for n in ("q_roped", "exp_done", "inv_done", "prob_done", "y_base"))

        def has(i):
            if not isinstance(i, int):
                return True, True, True, True
            return i < NG, i + 1 < NG, 1 <= i <= NG, i >= 2

        T_ORDER = ("q0", "q1", "q2", "x1n0", "x1n1", "q3", "p0", "tail0", "p1", "tail1", "p2", "tail2",
                   "xn0", "xn1", "p3", "tail3")
        M_ORDER = ("q1", "y0", "q2", "y1", "q3", "y2", "y3", "att0", "att1", "att2", "next_q0", "att3")

        def present(order, i):
            att, nxt, f1, y = has(i)
            stage = {"q": att, "p": att, "tail": att, "att": att, "xn": nxt, "next_q": nxt, "x1n": f1, "y": y}
            return [u for u in order if stage[u[:-1]]]

        def use(order, first, i, what):
            if isinstance(i, int):
                return first + sum(len(present(order, j)) for j in range(i)) + present(order, i).index(what)
            ahead = use(order, first, 2, what) - 2 * len(order)
            return i * len(order) + ahead

        def t_use(i, what):
            return use(T_ORDER, KD, i, what)

        def m_use(i, what):
            if what == "q0":
                return 0 if isinstance(i, int) and i == 0 else use(M_ORDER, 1, i - 1, "next_q0")
            return use(M_ORDER, 1, i, what)

        def bank(banks, uses, i, what):
            return banks[uses(i if isinstance(i, int) else 2, what) % 2]

        def t_bank(i, what):
            return bank(ps_t, t_use, i, what)

        def m_bank(i, what):
            return bank(ps_m, m_use, i, what)

        def last_bank(t):
            return (m_bank(NG + 1, "y0"), m_bank(NG + 1, "y1"), ps_t[0], ps_t[1])[t]

        def loop(eng, step):
            step(0, 0, 0)
            step(1, 1, 0)
            with eng.Fori(1, B - 1, 1) as b:
                step(b * 2, 0, b)
                step(b * 2 + 1, 1, b)
            for i in range(NG - 2, NG + 2):
                step(i, i % 2, i // 2)

        VW = [(b, h) for b in range(B) for h in (0, 2, None)]
        PIECE = NT * P
        PIECES = KD * F // PIECE

        def vw_at(i, place):
            kind, n = place
            if i == 0:
                return [n] if kind == "y" else {1: [4], 2: [5], 6: [6], 7: [7]}.get(n, [])
            return [2 * NT + n] if i == 1 and kind == "y" else []

        def pieces_at(i, place):
            kind, n = place
            if i == 0:
                return [n - 2] if kind == "h" and n >= 2 else []
            return [NF - 2 + n] if i == 1 and kind == "y" and n < 2 else []

        def vw_slot(dst, b, h):
            if h is None:
                return dst[:, b, H, :], slice(0, D)
            return dst[:, b, h:h + 2, :].rearrange("p a d -> p (a d)"), slice(0, 2 * D)

        def kk_parts(dst, rows, col):
            main = ps_s[0][rows, :].rearrange("p (b s) -> p b s", b=B)
            tails = ps_s[1][rows, 0:P].rearrange("p (b s) -> p b s", b=B)[:, :, 0:TAIL]
            return [(dst[rows, :, col:col + P], main), (dst[rows, :, col + P:col + S], tails)]

        block = ctx.enter_context(nc.Block())

        @block.sync
        def _(sp):
            sp.dma_start(ctx_sb[:, 0:B, :], ctx_main.rearrange("b p d -> p b d")).then_inc(ctx_in, 16)
            sp.wait_ge(ctx_zeroed, 1)
            for b in range(B):
                sp.dma_start(ctx_sb[TP * b:TP * b + TAIL, B, :], ctx_tail[b]).then_inc(ctx_in, 16)
            sp.dma_start(x_sb[0][:], x_g[0]).then_inc(x_in[0], 16)
            sp.dma_start(rq_cos[:], rope_q_cos).then_inc(rope_in, 16)
            sp.dma_start(rq_sin[:], rope_q_sin).then_inc(rope_in, 16)
            sp.dma_start(x_sb[1][:], x_g[1]).then_inc(x_in[1], 16)
            sp.dma_start(b1_sb[:], b1).then_inc(w_in, 16)
            sp.dma_start(w_raw[0][:].rearrange("p (k f) -> p k f", k=KD),
                         w1t.rearrange("(k p) f -> p k f", p=P)).then_inc(w_in, 16)
            sp.wait_ge(v_filled, 2)
            sp.wait_ge(kT_filled, 2)
            sp.dma_start(w_raw[1][:].rearrange("p (k f) -> p k f", k=NF),
                         w2t.rearrange("(k p) d -> p k d", p=P)).then_inc(w_in, 16)

            def step(i, p, b):
                att, _, _, y = has(i)
                if y:
                    sp.wait_ge(m_read, m_use(i, f"y{NT - 2}") + 1)
                    sp.dma_start(out_g[i - 2][:, 0:NT - 1], x1[p][:, 0:NT - 1]).then_inc(out_done[p], 16)
                    sp.wait_ge(m_read, m_use(i, f"y{NT - 1}") + 1)
                    sp.dma_start(out_g[i - 2][:, NT - 1], x1[p][:, NT - 1]).then_inc(last_out_done[p], 16)
                if att and not (isinstance(i, int) and i + 2 >= NG):
                    sp.wait_ge(bn2_done, i * NT + NT)
                    sp.dma_start(x_sb[p][:], x_g[i + 2]).then_inc(x_in[p], 16)

            loop(sp, step)
            for p in range(2):
                sp.wait_ge(out_done[p], 16 * B)
                sp.wait_ge(last_out_done[p], 16 * B)

        @block.gpsimd
        def _(pool):
            pool.memset(ctx_sb[:, B, :], 0.0).then_inc(ctx_zeroed, 1)
            pool.memset(neghalf[:], -0.5).then_inc(const_set, 1)
            pool.memset(ones_sb[:], 1.0).then_inc(const_set, 1)
            pool.dma_start(gate_raw[:, :], gates.partition_broadcast(P)).then_inc(gate_in, 16)
            pool.dma_start(mask_u8[:], mask.partition_broadcast(P)).then_inc(mask_in, 16)
            pool.dma_start(b2_raw, b2.partition_broadcast(P)).then_inc(b2_in, 16)

            pool.memset(prob_tail[:], 0.0).then_inc(zeros_set, 1)
            pool.memset(kk_hi[:].bitcast(F32), 0.0).then_inc(zeros_set, 1)
            pool.memset(kk_lo[:].bitcast(F32), 0.0).then_inc(zeros_set, 1)
            pool.memset(v_tail.bitcast(F32), 0.0).then_inc(zeros_set, 1)
            pool.wait_ge(ctx_stats, 1)
            pool.tensor_tensor(ctx_m2[:], ctx_mv[:, :, 0], ctx_mv[:, :, 0], ALU.mult).then_inc(ctx_ms_done, 1)
            pool.wait_ge(ctx_ms_done, 1)
            pool.tensor_tensor(ctx_ms[:], ctx_m2[:], ctx_mv[:, :, 1], ALU.add).then_inc(ctx_ms_done, 1)
            pool.wait_ge(ctx_ms_done, 2)
            pool.tensor_scalar(ctx_me[:], ctx_ms[:], RMS_EPS, None, ALU.add).then_inc(ctx_ms_done, 1)
            pool.wait_ge(ctx_ms_done, 3)
            pool.wait_ge(const_set, 1)
            pool.tensor_tensor(ctx_r[:], ctx_me[:], neghalf[:, 0:CT], ALU.pow).then_inc(ctx_rstd, 1)

            def rstd(ve, r, var_sem, rstd_sem, i):
                pool.wait_ge(var_sem, i + 1)
                pool.tensor_tensor(r[:], ve[:], neghalf[:, 0:NT], ALU.pow).then_inc(rstd_sem, 1)

            rstd(ve1, r1, ln1_var, ln1_rstd, 0)
            pool.wait_ge(wo_hi_set, 1)
            pool.tensor_tensor(wo_lo[:], wo_raw[:], wo_hi[:], ALU.subtract).then_inc(wo_set, 1)
            def rope_add(i, t):
                pool.wait_ge(m_read, m_use(i, f"q{t}") + 1)
                q = q_cos[t % 2]
                pool.tensor_tensor(q[:], q[:], q_sin[t % 2][:], ALU.add).then_inc(q_roped, 1)

            def step(i, p, b):
                att, nxt, f1, _ = has(i)

                first = isinstance(i, int) and i == 0

                def add_b2():
                    if f1:
                        pool.wait_ge(x1n_done, i * NT)
                        if isinstance(i, int) and i == 1:
                            pool.wait_ge(b2_set, 1)
                        b2s = b2_gated[:].rearrange("p (a d) -> p a d", a=1).to_broadcast([P, NT, D])
                        pool.tensor_tensor(x1[1 - p], x1[1 - p], b2s, ALU.add).then_inc(y_base, 1)

                def rstd2():
                    if f1:
                        rstd(ve2, r2, ln2_var, ln2_rstd, i - 1)

                if not att:
                    rstd2()
                    add_b2()
                    return

                def normalise(t):
                    pool.wait_ge(inv_done, i * NT + (t + 1))
                    inv = p_inv[:, t, :].rearrange("p (h a) -> p h a", a=1)
                    main, tail = prob[t][:, :, 0:P], prob[t][:, :, P:S]
                    pool.tensor_tensor(main, main, inv.to_broadcast([P, H, P]), ALU.mult)
                    pool.tensor_tensor(prob_tail[:, t, :, 0:TAIL], tail, inv.to_broadcast([P, H, TAIL]),
                                       ALU.mult).then_inc(prob_done, 1)

                rope_add(i, 1)
                rstd2()
                rope_add(i, 2)
                rope_add(i, 3)
                normalise(0)
                normalise(1)
                if first:
                    w_low_piece(0)
                normalise(2)
                if first:
                    w_low_piece(1)
                if nxt:
                    rstd(ve1, r1, ln1_var, ln1_rstd, i + 1)
                normalise(3)
                if first:
                    w_low_piece(2)
                add_b2()
                if first:
                    for n in range(3, 2 * PIECES):
                        w_low_piece(n)
                if nxt:
                    rope_add(i + 1, 0)

            rope_add(0, 0)
            pool.wait_ge(v_set, 2)
            pool.wait_ge(zeros_set, 4)
            for h in range(H):
                pool.tensor_copy(v_tail[:, :, h, TP * h:TP * (h + 1)],
                                 v_T[:, B * P:].rearrange("p (b j) -> p b j", b=B)).then_inc(v_tail_set, 1)

            def w_low_piece(n):
                m, cols = n // PIECES, slice(n % PIECES * PIECE, (n % PIECES + 1) * PIECE)
                if n == 0:
                    pool.wait_ge(w_thr_set, 2)
                if n >= NL:
                    pool.wait_ge(w_set, n - NL + 1)
                pool.tensor_scalar(w_low[n % NL], w_raw[m][:, cols], w_thr[:, 1, m:m + 1], None,
                                   ALU.is_lt).then_inc(w_low_set, 1)

            loop(pool, step)

        @block.scalar
        def _(act):
            act.dma_start(ident_sb[:], ident).then_inc(ident_in, 16)
            act.dma_start(scale_raw[:], rms_scale).then_inc(wkv_in, 16)
            act.dma_start(wkv_raw[:, :, 0, :], wk.rearrange("(k p) c -> p k c", p=P)).then_inc(wkv_in, 16)
            for j in (1, 2):
                act.dma_start(wkv_raw[:, :, j, :], wv.rearrange("(k p) c -> p k c", p=P)).then_inc(wkv_in, 16)
            act.dma_start(wq_raw[:], wq.rearrange("(k p) n -> p k n", p=P)).then_inc(wq_in, 16)
            act.dma_start(rk_cos[:], rope_k_cos).then_inc(tab_in, 16)
            act.dma_start(rk_sin[:], rope_k_sin).then_inc(tab_in, 16)
            for r in (0, C):
                act.dma_start(wo_raw[r:r + C], wo).then_inc(wo_in, 16)
            act.wait_ge(gate_in, 16)
            nc.scalar.activation(gate[:], gate_raw[:], ACT.Tanh).then_inc(gate_set, 1)
            for k in range(KD):
                act.wait_ge(ctxT_filled, k + 1)
                nc.scalar.activation(ctx_nT[:, k, 0:B * P], ps_s[k][:], ACT.Copy).then_inc(ctxT_copied, 1)
            act.wait_ge(ctxT_filled, 3)
            nc.scalar.activation(ctx_nT[:, :, B * P:], ps_h[0][:, 0:KD * P].rearrange("p (k s) -> p k s", k=KD),
                                 ACT.Copy).then_inc(ctxT_copied, 1)

            def hi_part(n, dst, src):
                act.wait_ge(t_filled, n + 1)
                nc.scalar.activation(dst, src, ACT.Copy).then_inc(t_hi, 1)

            act.wait_ge(wo_in, 32)
            nc.scalar.activation(wo_hi[:], wo_raw[:], ACT.Copy).then_inc(wo_hi_set, 1)
            for n, (cols, ps) in enumerate(((slice(0, B * P), ps_m[0][:]), (slice(B * P, CT * P), ps_m[1][:, 0:P]))):
                act.wait_ge(v_filled, n + 1)
                nc.scalar.activation(v_T[0:C, cols], ps[0:C], ACT.Copy).then_inc(v_hi_set, 1)
                nc.scalar.activation(v_tmp[C:P, cols], ps[C:P], ACT.Copy).then_inc(v_hi_set, 1)
            for k in range(KD):
                hi_part(k, xnT_hi[:, k, :], ps_t[k][:])
            act.wait_ge(kT_filled, 2)
            act.wait_ge(zeros_set, 3)
            for half in range(2):
                rows = slice(C * half, C * (half + 1))
                for dst, src in kk_parts(kk_hi, rows, S * half):
                    nc.scalar.activation(dst, src, ACT.Copy).then_inc(kk_hi_set, 1)
            def vw_hi_part(n):
                act.wait_ge(vw_filled, n + 1)
                dst, cols = vw_slot(vw_hi, *VW[n])
                nc.scalar.activation(dst, ps_h[n % 2][:, cols], ACT.Copy, scale=gate[:, 0:1]).then_inc(vw_hi_set, 1)

            def sum_weights(m):
                act.wait_ge(w_in, 16 * 3)
                if m:
                    act.wait_ge(w_summed, m)
                nc.scalar.activation(w_abs[:], w_raw[m][:, :], ACT.Abs, accum_out=w_sums[:, m:m + 1]).then_inc(w_summed, 1)

            def step(i, p, b):
                att, nxt, f1, _ = has(i)

                def q_hi(t):
                    hi_part(t_use(i, f"q{t}"), qT_hi[t % 2][:].rearrange("p a b -> p (a b)"), t_bank(i, f"q{t}")[:, 0:D])

                def norm2():
                    if f1:
                        act.wait_ge(ln2_shift, i)
                        for t in range(NT):
                            nc.scalar.activation(x1n[:, t, :], x1[1 - p][:, t, :], ACT.Identity,
                                                 scale=r2[:, t:t + 1], bias=mr2[:, t:t + 1]).then_inc(x1n_done, 1)

                def exps(t):
                    act.wait_ge(s_masked, i * NT + (t + 1))
                    for h in range(H):
                        e = nc.scalar.activation(prob[t][:, h, :], s_neg[t % 2][:, h, :], ACT.Exp,
                                                 bias=s_min[t % 2][:, h:h + 1], scale=-1.0,
                                                 accum_out=p_sum[:, t, h:h + 1])
                    e.then_inc(exp_done, 1)

                def p_hi(t):
                    if t < 2:
                        if not (isinstance(i, int) and i == 0):
                            act.wait_ge(m_filled, m_use(i - 1, f"att{t + 2}") + 1)
                    else:
                        act.wait_ge(m_filled, m_use(i, f"att{t - 2}") + 1)
                    hi_part(t_use(i, f"p{t}"), pT_hi[t % 2][:, 0:H, :].rearrange("p h s -> p (h s)"),
                            t_bank(i, f"p{t}")[:])
                    hi_part(t_use(i, f"tail{t}"), pT_hi[t % 2][:, H, :], t_bank(i, f"tail{t}")[:, 0:P])

                def setup_part(place):
                    if isinstance(i, int):
                        for n in vw_at(i, place):
                            vw_hi_part(n)

                def gelu(c):
                    setup_part(("h", c))
                    if not f1:
                        return
                    act.wait_ge(h_filled, i * NF + (c + 1 - NF))
                    if not (isinstance(i, int) and i == 1 and c < 4):
                        act.wait_ge(h_split, i * NF + (c - 3 - NF))
                    for dst in (h_act[c % 4][:], hT_hi[:, c, :]):
                        g = nc.scalar.activation(dst, ps_h[c % 2][:], ACT.Gelu, bias=b1_sb[:, c:c + 1])
                    g.then_inc(h_gelu, 1)

                def x1n_hi(k):
                    if f1:
                        hi_part(t_use(i, f"x1n{k}"), x1nT_hi[:, k, :], t_bank(i, f"x1n{k}")[:])

                def xn_hi():
                    if nxt:
                        for k in range(KD):
                            hi_part(t_use(i, f"xn{k}"), xnT_hi[:, k, :], t_bank(i, f"xn{k}")[:])

                if not att:
                    norm2()
                    for k in range(KD):
                        x1n_hi(k)
                    for c in range(NF):
                        gelu(c)
                    return
                q_hi(0)
                setup_part(("y", 0))
                nc.scalar.activation(exp_warm[:], neghalf[:, 0:1], ACT.Exp)
                if isinstance(i, int) and i == 0:
                    sum_weights(0)
                q_hi(1)
                setup_part(("y", 1))
                if isinstance(i, int) and i == 0:
                    sum_weights(1)
                norm2()
                q_hi(2)
                x1n_hi(0)
                exps(0)
                x1n_hi(1)
                setup_part(("y", 2))
                q_hi(3)
                exps(1)
                setup_part(("y", 3))
                exps(2)
                p_hi(0)
                exps(3)
                p_hi(1)
                gelu(0)
                gelu(1)
                p_hi(2)
                gelu(2)
                gelu(3)
                xn_hi()
                gelu(4)
                gelu(5)
                p_hi(3)
                for c in range(6, NF):
                    gelu(c)

            loop(act, step)

        @block.vector
        def _(dve):
            dve.wait_ge(ctx_in, 16 * (B + 1))
            for t in range(CT):
                dve.bn_stats(ctx_bn[:, t, :], ctx_sb[:, t, :]).then_inc(ctx_bn_done, 1)
            dve.wait_ge(ctx_bn_done, CT)
            for t in range(CT):
                s = dve.bn_aggr(ctx_mv[:, t, :], ctx_bn[:, t, :])
            s.then_inc(ctx_stats, 1)

            def sums1(p, b, tiles):
                if tiles[0] == 0:
                    dve.wait_ge(x_in[p], b * 16 + 16)
                for t in tiles:
                    dve.bn_stats(bn1[:, t, :], x_sb[p][:, t, :]).then_inc(bn1_done, 1)

            def variances(i, bn, mv, stats_sem, ve, var_sem, mul, add):
                for t in range(NT):
                    s = dve.bn_aggr(mv[:, t, :], bn[:, t, :])
                s.then_inc(stats_sem, 1)
                dve.wait_ge(stats_sem, i + 1)
                dve.tensor_scalar(ve[:], mv[:, :, 1], mul, add, ALU.mult, ALU.add).then_inc(var_sem, 1)

            def variances1(i):
                variances(i, bn1, mv1, ln1_stats, ve1, ln1_var, 1.0 + RMS_EPS, LN_EPS * RMS_EPS)

            def norm1(i, p):
                dve.wait_ge(ln1_rstd, i + 1)
                for t in range(NT):
                    dve.tensor_scalar(xn[:, t, :], x_sb[p][:, t, :], mv1[:, t, 0:1], r1[:, t:t + 1],
                                      ALU.subtract, ALU.mult).then_inc(xn_done, 1)

            def lo_part(n, dst, src, hi):
                dve.wait_ge(t_hi, n + 1)
                dve.tensor_tensor(dst, src, hi, ALU.subtract).then_inc(t_lo, 1)

            dve.wait_ge(wkv_in, 16 * 4)
            dve.tensor_scalar(scale1[:], scale_raw[:], 1.0, None, ALU.add).then_inc(scale1_set, 1)
            dve.wait_ge(scale1_set, 1)
            for k in range(KD):
                dve.tensor_scalar(wkv_s[:, k], wkv_raw[:, k], scale1[:, k:k + 1], None, ALU.mult).then_inc(wkv_scaled, 1)
            dve.wait_ge(ctx_rstd, 1)
            for t in range(CT):
                dve.tensor_scalar(ctx_n[:, t, :], ctx_sb[:, t, :], ctx_r[:, t:t + 1], None,
                                  ALU.mult).then_inc(ctx_normed, 1)
            sums1(0, 0, range(NT))
            dve.wait_ge(bn1_done, NT)
            variances1(0)
            dve.wait_ge(wq_in, 16)
            for k in range(KD):
                dve.tensor_scalar(wq_s[:, k], wq_raw[:, k], scale1[:, k:k + 1], None, ALU.mult).then_inc(wq_scaled, 1)
            dve.wait_ge(wq_scaled, KD)
            dve.tensor_copy(wq_hi[:], wq_s).then_inc(wq_hi_set, 1)
            norm1(0, 0)
            dve.wait_ge(k_filled, 1)
            dve.wait_ge(tab_in, 32)
            kps = ps_h[1][:, 0:CT * C].rearrange("p (t j c) -> p t j c", t=CT, j=2)
            for j in range(2):
                dve.tensor_tensor(k_a[:, :, j, :], kps[:, :, j, :], rk_cos[:], ALU.mult).then_inc(k_products, 1)
                dve.tensor_tensor(k_b[:, :, 1 - j, :], kps[:, :, j, :], rk_sin[:, :, j, :],
                                  ALU.mult).then_inc(k_products, 1)
            dve.wait_ge(k_products, 4)
            for j in range(2):
                dve.tensor_tensor(k_rot[:, :, j, :], k_a[:].rearrange("p t j c -> p t (j c)"),
                                  k_b[:].rearrange("p t j c -> p t (j c)"), ALU.add).then_inc(k_rotated, 1)
            dve.wait_ge(wq_hi_set, 1)
            dve.tensor_tensor(wq_lo[:], wq_s, wq_hi[:], ALU.subtract).then_inc(wq_set, 1)
            for n, (cols, ps) in enumerate(((slice(0, B * P), ps_m[0][:]), (slice(B * P, CT * P), ps_m[1][:, 0:P]))):
                dve.wait_ge(v_hi_set, 2 * n + 2)
                dve.tensor_tensor(v_T[C:P, cols], ps[C:P], v_tmp[C:P, cols], ALU.subtract).then_inc(v_set, 1)
            for k in range(KD):
                lo_part(k, xnT_lo[:, k, :], ps_t[k][:], xnT_hi[:, k, :])

            def rope(i, p, t):
                n = m_use(i, f"q{t}")
                dve.wait_ge(m_filled, n + 1)
                q = m_bank(i, f"q{t}")[:, 0:D]
                pos = NT * p + t
                cos = rq_cos[:, pos, :].rearrange("p (a c) -> p a c", a=1).to_broadcast([P, 2 * H, C // 2])
                dve.tensor_tensor(q_cos[t % 2][:].rearrange("p (a c) -> p a c", a=2 * H),
                                  q.rearrange("p (a c) -> p a c", a=2 * H), cos, ALU.mult)
                sin = rq_sin[:, pos].rearrange("p (a j) c -> p a j c", a=1).to_broadcast([P, H, 2, C // 2])
                dve.tensor_tensor(q_sin[t % 2][:].rearrange("p (h j c) -> p h j c", h=H, j=2)[:, :, ::-1, :],
                                  q.rearrange("p (h j c) -> p h j c", h=H, j=2), sin,
                                  ALU.mult).then_inc(m_read, 1)

            dve.wait_ge(rope_in, 32)
            rope(0, 0, 0)
            dve.wait_ge(kk_hi_set, 4)
            for half in range(2):
                rows = slice(C * half, C * (half + 1))
                for (dst, src), (hi, _) in zip(kk_parts(kk_lo, rows, S * half), kk_parts(kk_hi, rows, S * half)):
                    dve.tensor_tensor(dst, src, hi, ALU.subtract).then_inc(kk_set, 1)
            dve.wait_ge(mask_in, 16)
            dve.tensor_scalar(mask_bias[:], mask_u8[:], MASK_FILL, -MASK_FILL, ALU.mult, ALU.add).then_inc(mask_f_set, 1)
            dve.wait_ge(gate_set, 1)
            dve.wait_ge(b2_in, 16)
            dve.tensor_scalar(b2_gated[:], b2_raw, gate[:, 1:2], None, ALU.mult).then_inc(b2_set, 1)
            dve.wait_ge(mask_f_set, 1)

            def vw_lo_part(n):
                dve.wait_ge(vw_hi_set, n + 1)
                hi, cols = vw_slot(vw_hi, *VW[n])
                dve.scalar_tensor_tensor(vw_slot(vw_lo, *VW[n])[0], ps_h[n % 2][:, cols], gate[:, 0:1], hi,
                                         ALU.mult, ALU.subtract).then_inc(vw_set, 1)

            def weight_scales():
                dve.wait_ge(w_total, 1)
                dve.tensor_scalar(w_scale[:], ps_h[0][:, 0:2], 1.0 / (D * F), 1e-8, ALU.mult,
                                  ALU.max).then_inc(w_scaled, 1)
                dve.wait_ge(w_scaled, 1)
                for n, sign in enumerate((0.5, -0.5)):
                    dve.tensor_scalar(w_thr[:, n, :], w_scale[:], sign, None, ALU.mult).then_inc(w_thr_set, 1)

            def ternary(n):
                m, cols = n // PIECES, slice(n % PIECES * PIECE, (n % PIECES + 1) * PIECE)
                dve.wait_ge(w_low_set, n + 1)
                dve.scalar_tensor_tensor(w_tern[m][:, cols], w_raw[m][:, cols], w_thr[:, 0, m:m + 1], w_low[n % NL],
                                         ALU.is_gt, ALU.subtract).then_inc(w_set, 1)

            def step(i, p, b):
                att, nxt, f1, y = has(i)

                def q_lo(t):
                    lo_part(t_use(i, f"q{t}"), qT_lo[t % 2][:].rearrange("p a b -> p (a b)"),
                            t_bank(i, f"q{t}")[:, 0:D], qT_hi[t % 2][:].rearrange("p a b -> p (a b)"))

                def mask_and_min(t):
                    dve.wait_ge(s_filled, i * NT + (t + 1))
                    s, least = s_neg[t % 2], s_min[t % 2]
                    dve.tensor_tensor(s[:, 0, :], ps_s[0][:, 0:S], mask_now[:], ALU.add).then_inc(s_first, 1)
                    for h in range(1, H):
                        dve.tensor_tensor_reduce(
                            s[:, h, :], ps_s[h // 2][:, S * (h % 2):S * (h % 2 + 1)], mask_now[:],
                            1.0, 3.4e38, ALU.add, ALU.min, least[:, h:h + 1])
                    dve.wait_ge(s_first, i * NT + (t + 1))
                    dve.tensor_reduce(least[:, 0:1], s[:, 0, :], AX.X, ALU.min).then_inc(s_masked, 1)

                def inverse(t):
                    dve.wait_ge(exp_done, i * NT + (t + 1))
                    dve.reciprocal(p_inv[:, t, :], p_sum[:, t, :]).then_inc(inv_done, 1)

                def setup_part(place):
                    if not isinstance(i, int):
                        return
                    for n in vw_at(i, place):
                        vw_lo_part(n)
                    if i == 0 and place == ("y", NT - 1):
                        weight_scales()
                    for n in pieces_at(i, place):
                        ternary(n)

                def ffn_out(t):
                    setup_part(("y", t))
                    if not y:
                        return
                    n = m_use(i, f"y{t}")
                    dve.wait_ge(m_filled, n + 1)
                    dve.wait_ge(y_base, i - 1)
                    ys = x1[p][:, t, :]
                    last = isinstance(i, int) and i > NG
                    src = last_bank(t) if last else m_bank(i, f"y{t}")
                    dve.scalar_tensor_tensor(ys, src[:, 0:D], gate[:, 1:2], ys,
                                             ALU.mult, ALU.add).then_inc(m_read, 1)

                def p_lo(t):
                    lo_part(t_use(i, f"p{t}"), pT_lo[t % 2][:, 0:H, :].rearrange("p h s -> p (h s)"),
                            t_bank(i, f"p{t}")[:], pT_hi[t % 2][:, 0:H, :].rearrange("p h s -> p (h s)"))
                    lo_part(t_use(i, f"tail{t}"), pT_lo[t % 2][:, H, :], t_bank(i, f"tail{t}")[:, 0:P],
                            pT_hi[t % 2][:, H, :])

                def residual(t):
                    n = m_use(i, f"att{t}")
                    dve.wait_ge(m_filled, n + 1)
                    if t in (0, NT - 1) and not (isinstance(i, int) and i < 2):
                        dve.wait_ge((out_done if t == 0 else last_out_done)[p], b * 16)
                    dve.tensor_tensor(x1[p][:, t, :], m_bank(i, f"att{t}")[:, 0:D], x_sb[p][:, t, :],
                                      ALU.add).then_inc(m_read, 1)
                    dve.wait_ge(m_read, n + 1)
                    dve.bn_stats(bn2[:, t, :], x1[p][:, t, :]).then_inc(bn2_done, 1)

                def split_h(c):
                    setup_part(("h", c))
                    if not f1:
                        return
                    g = i * NF + (c + 1 - NF)
                    dve.wait_ge(h_gelu, g)
                    dve.tensor_tensor(hT_lo[:, c, :], h_act[c % 4][:], hT_hi[:, c, :], ALU.subtract).then_inc(h_split, 1)

                def x1n_lo(k):
                    if f1:
                        lo_part(t_use(i, f"x1n{k}"), x1nT_lo[:, k, :], t_bank(i, f"x1n{k}")[:], x1nT_hi[:, k, :])

                def xn_lo():
                    if nxt:
                        for k in range(KD):
                            lo_part(t_use(i, f"xn{k}"), xnT_lo[:, k, :], t_bank(i, f"xn{k}")[:], xnT_hi[:, k, :])

                def statistics2():
                    if f1:
                        variances(i - 1, bn2, mv2, ln2_stats, ve2, ln2_var, 1.0, LN_EPS)

                def shift2():
                    if f1:
                        """-mean * rstd of group i - 1."""
                        dve.wait_ge(ln2_rstd, i)
                        dve.scalar_tensor_tensor(mr2[:], mv2[:, :, 0], -1.0, r2[:], ALU.mult,
                                                 ALU.mult).then_inc(ln2_shift, 1)

                if not att:
                    if f1:
                        dve.wait_ge(bn2_done, i * NT)
                    statistics2()
                    shift2()
                    for t in range(NT - 1):
                        ffn_out(t)
                    for k in range(KD):
                        x1n_lo(k)
                    ffn_out(NT - 1)
                    for c in range(NF):
                        split_h(c)
                    return

                if f1:
                    dve.wait_ge(bn2_done, i * NT)
                q_lo(0)
                rope(i, p, 1)
                statistics2()
                if p == 0:
                    dve.tensor_copy(mask_now[:], mask_bias[:, b, :]).then_inc(mask_now_set, 1)
                ffn_out(0)
                if p == 0:
                    dve.wait_ge(mask_now_set, b + 1)
                mask_and_min(0)
                q_lo(1)
                shift2()
                rope(i, p, 2)
                ffn_out(1)
                mask_and_min(1)
                q_lo(2)
                rope(i, p, 3)
                x1n_lo(0)
                ffn_out(2)
                inverse(0)
                x1n_lo(1)
                mask_and_min(2)
                q_lo(3)
                inverse(1)
                ffn_out(3)
                mask_and_min(3)
                p_lo(0)
                inverse(2)
                if nxt:
                    sums1(1 - p, b + p, range(NT))
                    dve.wait_ge(bn1_done, i * NT + 2 * NT)
                p_lo(1)
                inverse(3)
                if nxt:
                    variances1(i + 1)
                residual(0)
                if nxt:
                    norm1(i + 1, 1 - p)
                p_lo(2)
                residual(1)
                split_h(0)
                split_h(1)
                split_h(2)
                xn_lo()
                split_h(3)
                residual(2)
                p_lo(3)
                split_h(4)
                split_h(5)
                if nxt:
                    rope(i + 1, 1 - p, 0)
                split_h(6)
                residual(3)
                split_h(7)

            loop(dve, step)

        @block.tensor
        def _(pe):
            def products(dst, pairs):
                for n, (lhs, rhs) in enumerate(pairs):
                    m = pe.matmul(dst, lhs, rhs, start=(n == 0), stop=(n == len(pairs) - 1))
                return m

            def transposed_tiles(n, dst, src, k):
                if not (isinstance(n, int) and n < 2):
                    pe.wait_ge(t_lo, n - 1)
                for t in range(NT):
                    m = pe.transpose(dst[:, P * t:P * (t + 1)], src[:, t, P * k:P * (k + 1)], ident_sb[:])
                m.then_inc(t_filled, 1)

            def keep_warm(n):
                for _ in range(n):
                    pe.matmul(ps_h[1][:, 0:P], ones_sb[:], ones_sb[:], start=True, stop=True)

            pe.wait_ge(const_set, 2)
            keep_warm(30)
            pe.wait_ge(ident_in, 16)
            pe.wait_ge(ctx_normed, CT)
            for k in range(KD):
                for t in range(B):
                    m = pe.transpose(ps_s[k][:, P * t:P * (t + 1)], ctx_n[:, t, P * k:P * (k + 1)], ident_sb[:])
                m.then_inc(ctxT_filled, 1)
            for k in range(KD):
                m = pe.transpose(ps_h[0][:, P * k:P * (k + 1)], ctx_n[:, B, P * k:P * (k + 1)], ident_sb[:])
            m.then_inc(ctxT_filled, 1)
            keep_warm(4)
            pe.wait_ge(wkv_scaled, KD)
            pe.wait_ge(ctxT_copied, 3)
            for t in range(CT):
                m = products(ps_h[1][:, C * t:C * (t + 1)],
                             [(ctx_nT[:, k, P * t:P * (t + 1)], wkv_s[:, k, 0, :]) for k in range(KD)])
            m.then_inc(k_filled, 1)
            for cols, dst in ((slice(0, B * P), ps_m[0][:]), (slice(B * P, CT * P), ps_m[1][:, 0:P])):
                products(dst, [(wkv_s[:, k, 1:3, :].rearrange("p a c -> p (a c)"), ctx_nT[:, k, cols])
                               for k in range(KD)]).then_inc(v_filled, 1)
            pe.wait_ge(xn_done, NT)
            for k in range(KD):
                transposed_tiles(k, ps_t[k], xn, k)
            pe.wait_ge(k_rotated, 2)
            for t in range(CT):
                dst = ps_s[0][:, P * t:P * (t + 1)] if t < B else ps_s[1][:, 0:P]
                m = pe.transpose(dst, k_rot[:, t].rearrange("p j c -> p (j c)"), ident_sb[:])
                if t >= B - 1:
                    m.then_inc(kT_filled, 1)
            pe.wait_ge(wq_set, 1)

            def vw_product(n):
                b, h = VW[n]
                if n == 0:
                    pe.wait_ge(wo_set, 1)
                if n == 2:
                    pe.wait_ge(v_tail_set, H)
                if n >= 2:
                    pe.wait_ge(vw_set, n - 1)
                if n == NT:
                    pe.wait_ge(w_scaled, 1)
                if h is None:
                    pairs = [(v_tail[:, b, j, :], w[:, j, :]) for w in (wo_hi, wo_lo) for j in range(H)]
                else:
                    pairs = [(v_T[:, P * b:P * (b + 1)], w[:, h:h + 2, :].rearrange("p a d -> p (a d)"))
                             for w in (wo_hi, wo_lo)]
                products(ps_h[n % 2][:, vw_slot(vw_hi, b, h)[1]], pairs).then_inc(vw_filled, 1)

            def total_weights():
                pe.wait_ge(w_summed, 2)
                pe.wait_ge(const_set, 2)
                pe.wait_ge(vw_set, NT - 1)
                pe.matmul(ps_h[0][:, 0:2], ones_sb[:], w_sums[:], start=True, stop=True).then_inc(w_total, 1)

            def bank_m(i, what):
                n = m_use(i, what)
                if not (isinstance(n, int) and n < 2):
                    pe.wait_ge(m_read, n - 1)
                return m_bank(i, what)[:, 0:D]

            def q(i, t):
                tile = slice(P * t, P * (t + 1))
                products(bank_m(i, f"q{t}"), [(a[:, k, tile], w[:, k, :]) for k in range(KD)
                                              for a, w in ((xnT_hi, wq_hi), (xnT_hi, wq_lo), (xnT_lo, wq_hi))]
                         ).then_inc(m_filled, 1)

            def step(i, p, b):
                att, nxt, f1, y = has(i)

                def setup_part(place):
                    if isinstance(i, int):
                        for n in vw_at(i, place):
                            vw_product(n)
                        if i == 0 and place == ("y", NT - 1):
                            total_weights()

                def q_T(t):
                    if not att:
                        return
                    n = t_use(i, f"q{t}")
                    pe.wait_ge(t_lo, n - 1)
                    pe.wait_ge(q_roped, i * NT + (t + 1))
                    for a in range(HP):
                        m = pe.transpose(t_bank(i, f"q{t}")[:, P * a:P * (a + 1)], q_cos[t % 2][:, P * a:P * (a + 1)],
                                         ident_sb[:])
                    m.then_inc(t_filled, 1)

                def scores(t):
                    if not att:
                        return
                    pe.wait_ge(t_lo, t_use(i, f"q{t}") + 1)
                    if isinstance(i, int) and i == 0 and t == 0:
                        pe.wait_ge(kk_set, 4)
                    else:
                        pe.wait_ge(s_masked, i * NT + t)
                    for a in range(HP):
                        m = products(ps_s[a][:, 0:2 * S],
                                     [(qT_hi[t % 2][:, a, :], kk_hi[:, b, :]), (qT_hi[t % 2][:, a, :], kk_lo[:, b, :]),
                                      (qT_lo[t % 2][:, a, :], kk_hi[:, b, :])])
                    m.then_inc(s_filled, 1)

                def p_T(t):
                    if not att:
                        return
                    pe.wait_ge(prob_done, i * NT + (t + 1))
                    n = t_use(i, f"p{t}")
                    pe.wait_ge(t_lo, n - 1)
                    for h in range(H):
                        m = pe.transpose(t_bank(i, f"p{t}")[:, P * h:P * (h + 1)], prob[t][:, h, 0:P], ident_sb[:])
                    m.then_inc(t_filled, 1)
                    pe.wait_ge(t_lo, n)
                    pe.transpose(t_bank(i, f"tail{t}")[:, 0:P], prob_tail[:, t].rearrange("p h s -> p (h s)"), ident_sb[:]).then_inc(t_filled, 1)

                def attend(t):
                    if not att:
                        return
                    pe.wait_ge(t_lo, t_use(i, f"tail{t}") + 1)
                    if isinstance(i, int) and i == 0 and t == 0:
                        pe.wait_ge(vw_set, 3)
                    dst = bank_m(i, f"att{t}")
                    hi, lo = pT_hi[t % 2], pT_lo[t % 2]
                    products(dst, [(a[:, c, :], w[:, b, c, :]) for c in range(H + 1)
                                   for a, w in ((hi, vw_hi), (hi, vw_lo), (lo, vw_hi))]).then_inc(m_filled, 1)

                def x1_T(k):
                    if f1:
                        if k == 0:
                            pe.wait_ge(x1n_done, i * NT)
                        transposed_tiles(t_use(i, f"x1n{k}"), t_bank(i, f"x1n{k}"), x1n, k)

                def ffn_in(c):
                    setup_part(("h", c))
                    if not f1:
                        return
                    if c == 0:
                        pe.wait_ge(t_lo, t_use(i, "x1n1") + 1)
                        if isinstance(i, int) and i == 1:
                            pe.wait_ge(w_set, 2 * PIECES)
                            pe.wait_ge(vw_set, len(VW))
                    if not (isinstance(i, int) and i == 1 and c < 2):
                        pe.wait_ge(h_gelu, i * NF + (c - 1 - NF))
                    w = w_tern[0][:].rearrange("p (k f) -> p k f", k=KD)
                    products(ps_h[c % 2][:], [(w[:, k, P * c:P * (c + 1)], a[:, k, :]) for k in range(KD)
                                              for a in (x1nT_hi, x1nT_lo)]).then_inc(h_filled, 1)

                def ffn_out(t):
                    setup_part(("y", t))
                    if not y:
                        return
                    w = w_tern[1][:].rearrange("p (c d) -> p c d", c=NF)
                    dst = bank_m(i, f"y{t}")
                    for c in range(NF):
                        if t == 0 and c in (0, NF - 2):
                            pe.wait_ge(h_split, (i - 1) * NF - (2 if c == 0 else 0))
                        for a in (hT_hi, hT_lo):
                            m = pe.matmul(dst, a[:, c, P * t:P * (t + 1)], w[:, c, :],
                                          start=(c == 0 and a is hT_hi), stop=(c == NF - 1 and a is hT_lo))
                    m.then_inc(m_filled, 1)

                def xn_T():
                    if nxt:
                        pe.wait_ge(xn_done, i * NT + 2 * NT)
                        for k in range(KD):
                            transposed_tiles(t_use(i, f"xn{k}"), t_bank(i, f"xn{k}"), xn, k)

                def last_out(t, chunks):
                    w = w_tern[1][:].rearrange("p (c d) -> p c d", c=NF)
                    for c in chunks:
                        if c == 0 and t < 2:
                            dst = bank_m(NG + 1, f"y{t}")
                        else:
                            dst = last_bank(t)[:, 0:D]
                        pe.wait_ge(h_split, (NG - 1) * NF + c + 1)
                        for a in (hT_hi, hT_lo):
                            m = pe.matmul(dst, a[:, c, P * t:P * (t + 1)], w[:, c, :],
                                          start=(c == 0 and a is hT_hi), stop=(c == NF - 1 and a is hT_lo))
                        if c == NF - 1:
                            m.then_inc(m_filled, 1)

                if not isinstance(i, int):
                    pass
                elif i == NG:
                    for t in range(NT - 1):
                        ffn_out(t)
                    for k in range(KD):
                        x1_T(k)
                    ffn_out(NT - 1)
                    for c in range(NF):
                        ffn_in(c)
                        if c >= 2:
                            for t in range(2):
                                last_out(t, [c - 2])
                    return
                elif i > NG:
                    last_out(2, range(NF - 2))
                    for c in (NF - 2, NF - 1):
                        for t in range(NT - 1):
                            last_out(t, [c])
                    last_out(NT - 1, range(NF))
                    return
                q(i, 1)
                if isinstance(i, int) and i == 0:
                    keep_warm(5)
                q_T(0)
                ffn_out(0)
                scores(0)
                q(i, 2)
                q_T(1)
                ffn_out(1)
                scores(1)
                q(i, 3)
                q_T(2)
                x1_T(0)
                ffn_out(2)
                x1_T(1)
                scores(2)
                q_T(3)
                ffn_out(3)
                scores(3)
                p_T(0)
                ffn_in(0)
                ffn_in(1)
                p_T(1)
                attend(0)
                attend(1)
                p_T(2)
                ffn_in(2)
                ffn_in(3)
                xn_T()
                ffn_in(4)
                ffn_in(5)
                attend(2)
                p_T(3)
                for c in range(6, NF):
                    ffn_in(c)
                if nxt:
                    pe.wait_ge(t_lo, t_use(i, "xn1") + 1)
                    q(i + 1, 0)
                attend(3)

            keep_warm(8)
            pe.wait_ge(v_set, 2)
            pe.wait_ge(t_lo, KD)
            q(0, 0)
            loop(pe, step)


def _rotation(positions, half):
    timescale = np.float32(MAX_WAVELENGTH) ** (np.float32(1.0 / half) * np.arange(half, dtype=np.float32))
    angle = positions.astype(np.float32)[..., None] / timescale.astype(np.float32)
    return np.cos(angle).astype(np.float32), np.sin(angle).astype(np.float32)


def kernel(x, ctx_1024, mask_BxS2_bk0, g_xattn, g_ffn, L0_xattn_rms_scale, L0_xattn_q_w, L0_xattn_kv_w,
           L0_xattn_out_w, L0_ffn_W1, L0_ffn_b1, L0_ffn_W2, L0_ffn_b2):
    import concourse.bacc as bacc
    from concourse.bass_utils import run_bass_kernel_spmd

    x, memory, mask = np.asarray(x), np.asarray(ctx_1024), np.asarray(mask_BxS2_bk0)
    q_w, kv_w, out_w = np.asarray(L0_xattn_q_w), np.asarray(L0_xattn_kv_w), np.asarray(L0_xattn_out_w)
    B, T, D = x.shape
    S = memory.shape[1]
    H, _, C = q_w.shape
    p, half = np.arange(P), C // 2

    q_cos, q_sin = _rotation(S + p[:, None] + P * np.arange(T // P)[None, :], half)
    k_pos = np.concatenate([np.repeat(p[:, None], B, 1), (P + p % 32)[:, None]], 1)
    k_cos, k_sin = _rotation(k_pos, half)
    power = np.float32(-(C ** -0.5))
    tables = {
        "rope_q_cos": q_cos, "rope_q_sin": np.stack([q_sin, -q_sin], 2),
        "rope_k_cos": k_cos * power, "rope_k_sin": np.stack([k_sin, -k_sin], 2) * power,
        "ident": np.eye(P, dtype=np.float32),
    }
    arrays = {
        "x": x,
        "ctx_main": memory[:, :P], "ctx_tail": memory[:, P:],
        "mask": mask,
        "gates": np.concatenate([np.asarray(g_xattn), np.asarray(g_ffn)]),
        "rms_scale": np.asarray(L0_xattn_rms_scale).reshape(D // P, P).T,
        "wq": q_w.transpose(1, 0, 2).reshape(D, H * C),
        "wk": kv_w[0, 0], "wv": kv_w[1, 0],
        "wo": out_w.transpose(1, 0, 2),
        "w1t": np.asarray(L0_ffn_W1).T, "b1": np.asarray(L0_ffn_b1).reshape(-1, P).T,
        "w2t": np.asarray(L0_ffn_W2).T, "b2": np.asarray(L0_ffn_b2),
        **tables,
    }
    arrays = {name: np.ascontiguousarray(a) for name, a in arrays.items()}
    nc = bacc.Bacc("TRN2", target_bir_lowering=False, num_devices=1)
    args = {name: nc.dram_tensor(f"in_{name}", a.shape, mybir.dt.from_np(a.dtype), kind="ExternalInput").ap()
            for name, a in arrays.items()}
    out = nc.dram_tensor("out_x", x.shape, F32, kind="ExternalOutput").ap()
    flamingo_block(nc, *args.values(), out)
    r = run_bass_kernel_spmd(nc, [{f"in_{name}": a for name, a in arrays.items()}], core_ids=[0])
    return r.results[0]["out_x"]
```
